# Optimizing a Trainium2 kernel written in Bass

```python
import numpy as np
import jax
import jax.numpy as jnp

def _softmax(x, axis=-1):
    return jax.nn.softmax(x, axis=axis)

def _gelu(x):
    return jax.nn.gelu(x, approximate=True)

def _silu(x):
    return jax.nn.silu(x)

def _sigmoid(x):
    return jax.nn.sigmoid(x)

def _layernorm(x, axis=-1, eps=1e-05):
    m = jnp.mean(x, axis=axis, keepdims=True)
    v = jnp.var(x, axis=axis, keepdims=True)
    return (x - m) / jnp.sqrt(v + eps)

def _scatter_add(tgt, idx, src, axis=0):
    return tgt.at[idx].add(src)

def _segment_sum(src, seg, n):
    return jax.ops.segment_sum(src, seg, n)
kernel_name = 'mk_seq_preln_d1_jaxref_r8_ceedd5'

def setup_inputs(seed: int=0):
    np.random.seed(seed)
    _w = jnp.asarray

    def _L0_attn_setup():
        import jax, jax.numpy as jnp
        import numpy as np
        DIM = 128
        HEADS = 16
        HEAD_DIM = 64
        WINDOW = 64
        key = jax.random.key(seed)
        ks = jax.random.split(key, 9)
        s = lambda fan_in: 1.0 / np.sqrt(fan_in)
        x = jax.random.normal(ks[0], (2, 256, DIM), dtype=jnp.float32)
        W1 = jax.random.uniform(ks[1], (DIM, DIM), jnp.float32, -s(DIM), s(DIM))
        b1 = jax.random.uniform(ks[2], (DIM,), jnp.float32, -s(DIM), s(DIM))
        W2 = jax.random.uniform(ks[3], (DIM, DIM), jnp.float32, -s(DIM), s(DIM))
        b2 = jax.random.uniform(ks[4], (DIM,), jnp.float32, -s(DIM), s(DIM))
        Wg = jax.random.uniform(ks[5], (3 * HEADS * HEAD_DIM, DIM), jnp.float32, -s(DIM), s(DIM))
        bg = jax.random.uniform(ks[6], (3 * HEADS * HEAD_DIM,), jnp.float32, -s(DIM), s(DIM))
        Wo = jax.random.uniform(ks[7], (DIM, HEADS * HEAD_DIM), jnp.float32, -s(HEADS * HEAD_DIM), s(HEADS * HEAD_DIM))
        bo = jax.random.uniform(ks[8], (DIM,), jnp.float32, -s(HEADS * HEAD_DIM), s(HEADS * HEAD_DIM))
        return {'x': x, 'W1': W1, 'b1': b1, 'W2': W2, 'b2': b2, 'Wg': Wg, 'bg': bg, 'Wo': Wo, 'bo': bo}
    _L0_attn_in = _L0_attn_setup()

    def _L0_ffn_setup():
        import jax, jax.numpy as jnp
        import numpy as np
        N_EMBD = 128
        N_STATE = 512
        key = jax.random.key(seed)
        k_x, k_w1, k_b1, k_w2, k_b2 = jax.random.split(key, 5)
        x = jax.random.normal(k_x, (4, 256, N_EMBD), dtype=jnp.float32)
        w1 = jax.random.normal(k_w1, (N_EMBD, N_STATE), dtype=jnp.float32) * (1.0 / np.sqrt(N_EMBD))
        b1 = jax.random.normal(k_b1, (N_STATE,), dtype=jnp.float32) * 0.02
        w2 = jax.random.normal(k_w2, (N_STATE, N_EMBD), dtype=jnp.float32) * (1.0 / np.sqrt(N_STATE))
        b2 = jax.random.normal(k_b2, (N_EMBD,), dtype=jnp.float32) * 0.02
        return {'x': x, 'w1': w1, 'b1': b1, 'w2': w2, 'b2': b2}
    _L0_ffn_in = _L0_ffn_setup()
    _d = {'L0_attn_x': _L0_attn_in['x'], 'L0_attn_W1': _L0_attn_in['W1'], 'L0_attn_b1': _L0_attn_in['b1'], 'L0_attn_W2': _L0_attn_in['W2'], 'L0_attn_b2': _L0_attn_in['b2'], 'L0_attn_Wg': _L0_attn_in['Wg'], 'L0_attn_bg': _L0_attn_in['bg'], 'L0_attn_Wo': _L0_attn_in['Wo'], 'L0_attn_bo': _L0_attn_in['bo'], 'L0_ffn_w1': _L0_ffn_in['w1'], 'L0_ffn_b1': _L0_ffn_in['b1'], 'L0_ffn_w2': _L0_ffn_in['w2'], 'L0_ffn_b2': _L0_ffn_in['b2']}
    _x0 = _d['L0_attn_x']
    _d['L0_attn_x'] = jax.random.normal(jax.random.fold_in(jax.random.key(seed), 1), (32, 256, 128), dtype=_x0.dtype)
    del _x0
    return _d

def reference(L0_attn_x, L0_attn_W1, L0_attn_b1, L0_attn_W2, L0_attn_b2, L0_attn_Wg, L0_attn_bg, L0_attn_Wo, L0_attn_bo, L0_ffn_w1, L0_ffn_b1, L0_ffn_w2, L0_ffn_b2):

    def _L0_attn_ref(x, W1, b1, W2, b2, Wg, bg, Wo, bo):
        import jax, jax.numpy as jnp
        import numpy as np
        DIM = 128
        HEADS = 16
        HEAD_DIM = 64
        WINDOW = 64
        b, n, _ = x.shape
        h = jax.nn.silu(x @ W1.T + b1) @ W2.T + b2
        qkv = h @ Wg.T + bg
        q, k, v = jnp.split(qkv, 3, axis=-1)
        reshape = lambda t: t.reshape(b, n, HEADS, HEAD_DIM).transpose(0, 2, 1, 3)
        q, k, v = (reshape(q), reshape(k), reshape(v))
        dots = jnp.einsum('bhid,bhjd->bhij', q, k) * HEAD_DIM ** (-0.5)
        i = jnp.arange(n)[:, None]
        j = jnp.arange(n)[None, :]
        mask = j >= i + WINDOW
        dots = jnp.where(mask, -jnp.inf, dots)
        attn = jax.nn.softmax(dots, axis=-1)
        out = jnp.einsum('bhij,bhjd->bhid', attn, v)
        out = out.transpose(0, 2, 1, 3).reshape(b, n, HEADS * HEAD_DIM)
        return out @ Wo.T + bo

    def _L0_ffn_ref(x, w1, b1, w2, b2):
        import jax, jax.numpy as jnp
        import numpy as np
        N_EMBD = 128
        N_STATE = 512
        h = jax.nn.gelu(jnp.einsum('bse,eh->bsh', x, w1) + b1, approximate=False)
        return jnp.einsum('bsh,he->bse', h, w2) + b2
    x = L0_attn_x
    x = x + _L0_attn_ref(_layernorm(x, axis=-1), L0_attn_W1, L0_attn_b1, L0_attn_W2, L0_attn_b2, L0_attn_Wg, L0_attn_bg, L0_attn_Wo, L0_attn_bo)
    x = x + _L0_ffn_ref(_layernorm(x, axis=-1), L0_ffn_w1, L0_ffn_b1, L0_ffn_w2, L0_ffn_b2)
    return x

_drawn_inputs = setup_inputs


def setup_inputs(seed=0):
    import zlib

    import numpy as np

    out = dict(_drawn_inputs(seed))
    spreads = {}
    factors = {'L0_attn_W1': 8.0,
     'L0_attn_b1': 8.0,
     'L0_attn_W2': 3.973,
     'L0_attn_b2': 2.733,
     'L0_attn_bo': 8.197,
     'L0_ffn_b1': 5.085,
     'L0_ffn_b2': 3.33}
    for name, (base, spread) in spreads.items():
        noise = np.random.default_rng([zlib.crc32(name.encode()), seed]).standard_normal(out[name].shape)
        drawn = base * np.exp(spread * noise) if base else spread * noise
        out[name] = jnp.asarray(drawn.astype(out[name].dtype))
    for name, factor in factors.items():
        out[name] = (out[name] * factor).astype(out[name].dtype)
    return out
```

```python
from contextlib import ExitStack

import concourse.bass as bass
from concourse import mybir

F32 = mybir.dt.float32
F32R = mybir.dt.float32r
ACT = mybir.ActivationFunctionType
ALU = mybir.AluOpType

P = 128
BATCH, SEQ, DIM = 32, 256, 128
HEADS, HEAD_DIM, WINDOW = 16, 64, 64
HIDDEN = 512
PAIRS = HEADS // 2
GROUP = 2 * SEQ
BLOCKS = GROUP // P
GROUPS = BATCH * SEQ // GROUP
SLOTS = 2 * PAIRS
HCHUNKS = HIDDEN // P
SCALE = HEAD_DIM ** -0.5
EPS = 1e-5
MASKED = -3.0e38

KEYS = [min(SEQ, P * (i + 1) + WINDOW) for i in range(2)]
S_OFF = [0, KEYS[0]]
S_COLS = sum(KEYS)
PT_FROM = P - WINDOW

B_QKV, B_1, B_2, B_O, B_F1, B_F2 = 0, 24, 25, 26, 27, 31
N_BIAS = 32
W_1, W_2, W_G, W_O, W_F1, W_F2 = 0, 128, 256, 3328, 4352, 4864
N_W = 5376


def preln_block(nc, x, w1t, w2t, wgt, wot, fw1, fw2, biases, out):
    ctx = ExitStack()
    with ctx:
        def sb(name, shape, dt=F32):
            return ctx.enter_context(nc.sbuf_tensor(name, shape, dt))

        def sem(name):
            return ctx.enter_context(nc.semaphore(name))

        x_all = sb("x_all", [P, GROUPS * BLOCKS * DIM])
        bias = sb("bias", [P, N_BIAS])
        neg_b1 = sb("neg_b1", [P, 1])
        w_hi = sb("w_hi", [P, N_W], F32R)
        w_lo = sb("w_lo", [P, N_W], F32R)
        work = sb("work", [P, 12 * 512])
        w_raw = work[:, 0:N_W]
        probs = work[:, 0:8 * 512].rearrange("p (r h c) -> p r h c", r=4, h=2)
        probs_t = work[:, 8 * 512:12 * 512].rearrange("p (r h c) -> p r h c", r=2, h=2)
        ident = sb("ident", [P, P])
        mask = sb("mask", [P, S_COLS])
        stats = sb("stats", [P, BLOCKS, 6])
        mean_var = sb("mean_var", [P, BLOCKS, 2])
        var_eps = sb("var_eps", [P, BLOCKS])
        rstd = sb("rstd", [P, BLOCKS])
        minus_half = sb("minus_half", [P, BLOCKS])
        xn = sb("xn", [P, BLOCKS, DIM])
        xnt_hi = sb("xnt_hi", [P, GROUP], F32R)
        xnt_lo = sb("xnt_lo", [P, GROUP], F32R)
        z1 = sb("z1", [P, GROUP])
        e1 = sb("e1", [P, GROUP])
        s_hi = sb("s_hi", [P, GROUP], F32R)
        s_lo = sb("s_lo", [P, GROUP], F32R)
        h_hi = sb("h_hi", [P, GROUP], F32R)
        h_lo = sb("h_lo", [P, GROUP], F32R)
        q_hi = sb("q_hi", [P, 2, GROUP], F32R)
        q_lo = sb("q_lo", [P, 2, GROUP], F32R)
        k_hi = sb("k_hi", [P, 2, 2, GROUP], F32R)
        k_lo = sb("k_lo", [P, 2, 2, GROUP], F32R)
        v = sb("v", [P, BLOCKS, HEADS * HEAD_DIM])
        o_hi = sb("o_hi", [P, PAIRS, GROUP], F32R)
        o_lo = sb("o_lo", [P, PAIRS, GROUP], F32R)
        y = sb("y", [P, GROUP])
        row_max = sb("row_max", [P, 4, 4])
        neg_max = sb("neg_max", [P, 4, 4])
        row_sum = sb("row_sum", [P, 4, 4])
        inv_sum = sb("inv_sum", [P, 4, 4])
        g_f32 = [z1, e1]

        bank = [ctx.enter_context(nc.psum_tensor(f"bank{i}", [P, 512], F32)) for i in range(8)]
        s_ps = bank[0:4]
        t_ps = bank[4:6]
        pv_ps = bank[6]
        misc = bank[7]

        x_in, x_rest_in, w12_in, wg_in, wof_in, bias_in = map(
            sem, ("x_in", "x_rest_in", "w12_in", "wg_in", "wof_in", "bias_in"))
        consts_ready = sem("consts_ready")
        zeros_ready = sem("zeros_ready")
        w_hi_ready = sem("w_hi_ready")
        w_ready = sem("w_ready")
        stats_done, mv_ready = sem("stats_done"), sem("mv_ready")
        rstd_step, rstd_ready, xn_ready = sem("rstd_step"), sem("rstd_ready"), sem("xn_ready")
        tx_done, xnt_hi_ready, xnt_ready = sem("tx_done"), sem("xnt_hi_ready"), sem("xnt_ready")
        m1_done, e1_ready, silu_step, s_ready = sem("m1_done"), sem("e1_ready"), sem("silu_step"), sem("s_ready")
        m2_done, h_hi_ready, h_ready = sem("m2_done"), sem("h_hi_ready"), sem("h_ready")
        q_done, q_hi_ready, q_ready = sem("q_done"), sem("q_hi_ready"), sem("q_ready")
        k_done, k_hi_ready, k_ready = sem("k_done"), sem("k_hi_ready"), sem("k_ready")
        v_done, v_ready = sem("v_done"), sem("v_ready")
        s_done = sem("s_done")
        max_done, neg_ready = sem("max_done"), sem("neg_ready")
        exp_done, inv_ready, norm_done = sem("exp_done"), sem("inv_ready"), sem("norm_done")
        t_done = sem("t_done")
        pt_ready = [sem("pt0_ready"), sem("pt1_ready")]
        pv_done, o_hi_ready, o_ready = sem("pv_done"), sem("o_hi_ready"), sem("o_ready")
        om_done, y_ready, ty_done, x1_ready = sem("om_done"), sem("y_ready"), sem("ty_done"), sem("x1_ready")
        f_stats, f_mv, f_rstd_step = sem("f_stats"), sem("f_mv"), sem("f_rstd_step")
        f_rstd, f_xn = sem("f_rstd"), sem("f_xn")
        f_tx, f_xnt_hi, f_xnt = sem("f_tx"), sem("f_xnt_hi"), sem("f_xnt")
        f_m1, f_gelu, f_g_hi, f_g = sem("f_m1"), sem("f_gelu"), sem("f_g_hi"), sem("f_g")
        f_m2, f_y, f_ty, f_out = sem("f_m2"), sem("f_y"), sem("f_ty"), sem("f_out")
        stored = sem("stored")
        dve_passed, pool_passed = sem("dve_passed"), sem("pool_passed")

        def split_product(eng, out_ap, w, a, first=True, last=True):
            eng.matmul(out_ap, w[0], a[0], start=first, stop=False)
            eng.matmul(out_ap, w[0], a[1], start=False, stop=False)
            return eng.matmul(out_ap, w[1], a[0], start=False, stop=last)

        def w_parts(at, n=P):
            return w_hi[:, at:at + n], w_lo[:, at:at + n]

        def x_group(it):
            return x_all[:, bass.ds(it * (BLOCKS * DIM), BLOCKS * DIM)]

        def x_block(it, b):
            return x_all[:, bass.ds(it * (BLOCKS * DIM) + b * DIM, DIM)]

        x_v = x.rearrange("(n p) d -> p n d", p=P)
        out_v = out.rearrange("(n p) d -> p n d", p=P)
        block = ctx.enter_context(nc.Block())

        def task_a(s):
            pair = s // 2 + 1
            return ("q", "k")[s % 2], pair // PAIRS, pair % PAIRS

        TASK_B = {0: ("v", 0, 2), 1: ("v", 0, 3), 3: ("om", -1, 0), 4: ("v", 0, 4), 5: ("v", 0, 5),
                  6: ("v", 0, 6), 7: ("v", 0, 7), 8: ("ty", -1, 0), 9: ("tx", 1, 0), 11: ("m1", 1, 0),
                  13: ("m2", 1, 0), 14: ("v", 1, 0), 15: ("v", 1, 1)}

        def present(task, first, last):
            return task is not None and not (first and task[1] < 0) and not (last and task[1] > 0)

        @block.sync
        def _(sp):
            sp.dma_start(x_all[:, 0:BLOCKS * DIM].rearrange("p (n d) -> p n d", d=DIM),
                         x_v[:, 0:BLOCKS, :]).then_inc(x_in, 16)
            sp.dma_start(w_raw[:, W_1:W_1 + P], w1t).then_inc(w12_in, 16)
            sp.dma_start(w_raw[:, W_2:W_2 + P], w2t).then_inc(w12_in, 16)
            sp.dma_start(bias[:, :], biases).then_inc(bias_in, 16)
            sp.dma_start(w_raw[:, W_G:W_O], wgt).then_inc(wg_in, 16)
            sp.dma_start(w_raw[:, W_O:W_F1], wot).then_inc(wof_in, 16)
            sp.dma_start(w_raw[:, W_F1:W_F2], fw1).then_inc(wof_in, 16)
            sp.dma_start(w_raw[:, W_F2:N_W], fw2).then_inc(wof_in, 16)
            sp.dma_start(x_all[:, BLOCKS * DIM:].rearrange("p (n d) -> p n d", d=DIM),
                         x_v[:, BLOCKS:, :]).then_inc(x_rest_in, 16)

            def store(c):
                sp.wait_ge(f_out, c + 1)
                sp.dma_start(out_v[:, bass.ds(c * BLOCKS, BLOCKS), :],
                             x_group(c).rearrange("p (n d) -> p n d", d=DIM)).then_inc(stored, 16)

            with sp.Fori(0, GROUPS) as c:
                store(c)
            sp.wait_ge(stored, 16 * GROUPS)

        @block.gpsimd
        def _(pool):
            pool.memset(ident[:, :], 0.0)
            pool.memset(minus_half[:, :], -0.5)
            pool.memset(mask[:, :], 0.0).then_inc(consts_ready, 1)
            pool.wait_ge(consts_ready, 1)
            pool.affine_select(out=ident[:, :], in_=ident[:, :], compare_op=ALU.not_equal, fill=1.0,
                               base=0, pattern=[[-1, P]], channel_multiplier=1)
            for i in range(2):
                m = mask[:, S_OFF[i]:S_OFF[i] + KEYS[i]]
                last = pool.affine_select(out=m, in_=m, compare_op=ALU.is_ge, fill=MASKED,
                                          base=P * i + WINDOW - 1, pattern=[[-1, KEYS[i]]],
                                          channel_multiplier=1)
            last.then_inc(consts_ready, 1)

            def inverse_deviations(n, moments, step, ready):
                pool.wait_ge(moments, n + 1)
                pool.sem_inc(pool_passed, 1)
                pool.tensor_scalar(var_eps[:, :], mean_var[:, :, 1], EPS, 1.0, ALU.add,
                                   ALU.mult).then_inc(step, 1)
                pool.wait_ge(step, n + 1)
                pool.tensor_tensor(rstd[:, :], var_eps[:, :], minus_half[:, :], ALU.pow).then_inc(ready, 1)

            def normalise(g, s):
                pool.wait_ge(inv_ready, g + 1)
                pool.sem_inc(pool_passed, 1)
                for hd in range(2):
                    for i in range(2):
                        a = probs[:, s % 4, hd, SEQ * i:SEQ * i + KEYS[i]]
                        last = pool.tensor_scalar(a, a, inv_sum[:, s % 4, 2 * hd + i:2 * hd + i + 1], 1.0,
                                                  ALU.mult, ALU.mult)
                last.then_inc(norm_done, 1)

            def group(it, first=False, last=False):
                for s in range(SLOTS):
                    if not (first and s == 0):
                        normalise(it * SLOTS + s - 1, (s - 1) % SLOTS)
                    if s == 7 and not last:
                        inverse_deviations(it + 1, mv_ready, rstd_step, rstd_ready)

            inverse_deviations(0, mv_ready, rstd_step, rstd_ready)
            group(0, first=True)
            with pool.Fori(1, GROUPS - 1) as it:
                group(it)
            group(GROUPS - 1, last=True)
            normalise(GROUPS * SLOTS - 1, SLOTS - 1)

            with pool.Fori(0, GROUPS) as c:
                inverse_deviations(c, f_mv, f_rstd_step, f_rstd)

        @block.tensor
        def _(pe):
            def free(task):
                kind, it, i = task
                if kind in "qkv":
                    pe.wait_ge({"q": q_ready, "k": k_ready, "v": v_ready}[kind], it * 8 + i + 1)
                else:
                    pe.wait_ge({"tx": xnt_ready, "m1": s_ready, "m2": h_ready, "om": y_ready,
                                "ty": x1_ready}[kind], it + 1)

            def do(task):
                kind, it, i = task
                if kind == "tx":
                    pe.wait_ge(xn_ready, it + 1)
                    for b in range(BLOCKS):
                        last = pe.transpose(misc[:, b * P:(b + 1) * P], xn[:, b, :], ident[:, :])
                    last.then_inc(tx_done, 1)
                elif kind == "m1":
                    pe.wait_ge(xnt_ready, it + 1)
                    split_product(pe, misc[:, :], w_parts(W_1), (xnt_hi[:, :], xnt_lo[:, :])).then_inc(m1_done, 1)
                elif kind == "m2":
                    pe.wait_ge(s_ready, it + 1)
                    split_product(pe, misc[:, :], w_parts(W_2), (s_hi[:, :], s_lo[:, :])).then_inc(m2_done, 1)
                elif kind in "qk":
                    pe.wait_ge(h_ready, it + 1)
                    at = W_G + (kind == "k") * HEADS * HEAD_DIM + i * P
                    split_product(pe, misc[:, :], w_parts(at), (h_hi[:, :], h_lo[:, :])).then_inc(
                        q_done if kind == "q" else k_done, 1)
                elif kind == "v":
                    pe.wait_ge(h_ready, it + 1)
                    b, at = i % 4, W_G + 2 * HEADS * HEAD_DIM + i // 4 * 512
                    cols = slice(b * P, (b + 1) * P)
                    split_product(pe, misc[:, :], (h_hi[:, cols], h_lo[:, cols]),
                                  w_parts(at, 512)).then_inc(v_done, 1)
                elif kind == "om":
                    pe.wait_ge(o_ready, (it + 1) * SLOTS)
                    for p in range(PAIRS):
                        last = split_product(pe, misc[:, :], w_parts(W_O + p * P), (o_hi[:, p, :], o_lo[:, p, :]),
                                             first=p == 0, last=p == PAIRS - 1)
                    last.then_inc(om_done, 1)
                elif kind == "ty":
                    pe.wait_ge(y_ready, it + 1)
                    for b in range(BLOCKS):
                        last = pe.transpose(misc[:, b * P:(b + 1) * P], y[:, b * P:(b + 1) * P], ident[:, :])
                    last.then_inc(ty_done, 1)

            def scores(it, s, first):
                g, p, b = it * SLOTS + s, s // 2, s % 2
                pe.wait_ge(q_ready, it * 8 + p + 1)
                pe.wait_ge(k_ready, it * 8 + p + 1)
                if not (first and s < 2):
                    pe.wait_ge(exp_done, g - 1)
                for hd in range(2):
                    for i in range(2):
                        dst = s_ps[2 * (s % 2) + hd][:, S_OFF[i]:S_OFF[i] + KEYS[i]]
                        rows = slice(b * SEQ + i * P, b * SEQ + (i + 1) * P)
                        cols = slice(b * SEQ, b * SEQ + KEYS[i])
                        last = split_product(pe, dst, (q_hi[:, p % 2, rows], q_lo[:, p % 2, rows]),
                                             (k_hi[:, p % 2, hd, cols], k_lo[:, p % 2, hd, cols]))
                    last.then_inc(s_done, 1)

            def transposes(it, s, first):
                g = it * SLOTS + s
                pe.wait_ge(norm_done, g + 1)
                for hd in range(2):
                    if not (first and s == 0):
                        pe.wait_ge(pt_ready[hd], g)
                    for n, j in enumerate((1, 0)):
                        for i in range(2):
                            last = pe.transpose(t_ps[hd][:, SEQ * n + P * i:SEQ * n + P * (i + 1)],
                                                probs[:, s % 4, hd, SEQ * i + P * j:SEQ * i + P * (j + 1)],
                                                ident[:, :])
                    last.then_inc(t_done, 1)

            def values(it, s, first):
                g, p, b = it * SLOTS + s, s // 2, s % 2
                for hd in range(2):
                    pe.wait_ge(pt_ready[hd], g + 1)
                pe.wait_ge(v_ready, it * 8 + p // 4 * 4 + 2 * b + 2)
                if not (first and s == 0):
                    pe.wait_ge(o_ready, g)
                for j in range(2):
                    for hd in range(2):
                        head = (2 * p + hd) * HEAD_DIM
                        dst = pv_ps[hd * HEAD_DIM:(hd + 1) * HEAD_DIM, PT_FROM * j:SEQ]
                        src = probs_t[:, s % 2, hd, (SEQ, PT_FROM)[j]:(2 * SEQ, SEQ)[j]]
                        last = pe.matmul(dst, v[:, 2 * b + j, head:head + HEAD_DIM], src,
                                         start=j == 0, stop=j == 1)
                last.then_inc(pv_done, 1)

            def group(it, prev, first=False, last=False):
                for s in range(SLOTS):
                    scores(it, s, first)
                    kind, ahead, i = task_a(s)
                    if not (last and ahead):
                        free(prev)
                        prev = (kind, it + ahead, i)
                        do(prev)
                    before, same = (it, True) if s >= 2 else (it - 1, False)
                    if same or not first:
                        transposes(before, (s - 2) % SLOTS, first and same)
                    b_task = TASK_B.get(s)
                    if present(b_task, first, last) and b_task[0] == "om":
                        free(prev)
                        prev = (b_task[0], it + b_task[1], b_task[2])
                        do(prev)
                    before, same = (it, True) if s >= 3 else (it - 1, False)
                    if same or not first:
                        values(before, (s - 3) % SLOTS, first and same)
                    if present(b_task, first, last) and b_task[0] != "om":
                        free(prev)
                        prev = (b_task[0], it + b_task[1], b_task[2])
                        do(prev)
                return prev

            pe.wait_ge(consts_ready, 2)
            do(("tx", 0, 0))
            pe.wait_ge(w_ready, 1)
            do(("m1", 0, 0))
            do(("m2", 0, 0))
            pe.wait_ge(w_ready, 2)
            do(("q", 0, 0))
            free(("q", 0, 0))
            do(("k", 0, 0))
            free(("k", 0, 0))
            do(("v", 0, 0))
            free(("v", 0, 0))
            do(("v", 0, 1))
            pe.wait_ge(w_ready, 3)
            pe.wait_ge(zeros_ready, 1)
            group(0, ("v", 0, 1), first=True)
            with pe.Fori(1, GROUPS - 1) as it:
                group(it, ("v", it, 1))
            end = GROUPS - 1
            prev = group(end, ("v", end, 1), last=True)
            transposes(end, SLOTS - 2, False)
            values(end, SLOTS - 3, False)
            transposes(end, SLOTS - 1, False)
            values(end, SLOTS - 2, False)
            values(end, SLOTS - 1, False)
            free(prev)
            do(("om", end, 0))
            do(("ty", end, 0))
            free(("ty", end, 0))

            def f_transpose_x(c):
                pe.wait_ge(f_xn, c + 1)
                for b in range(BLOCKS):
                    last = pe.transpose(bank[0][:, b * P:(b + 1) * P], xn[:, b, :], ident[:, :])
                last.then_inc(f_tx, 1)

            def f_hidden(c, k):
                if k == 0:
                    pe.wait_ge(f_xnt, c + 1)
                split_product(pe, bank[1 + k][:, :], w_parts(W_F1 + k * P),
                              (xnt_hi[:, :], xnt_lo[:, :])).then_inc(f_m1, 1)

            def f_down(c, k):
                pe.wait_ge(f_g, c * HCHUNKS + k + 1)
                last = split_product(pe, bank[5][:, :], w_parts(W_F2 + k * P), (o_hi[:, k, :], o_lo[:, k, :]),
                                     first=k == 0, last=k == HCHUNKS - 1)
                if k == HCHUNKS - 1:
                    last.then_inc(f_m2, 1)

            def f_transpose_y(c):
                pe.wait_ge(f_y, c + 1)
                if not (isinstance(c, int) and c < 1):
                    pe.wait_ge(f_out, c)
                for b in range(BLOCKS):
                    last = pe.transpose(bank[6][:, b * P:(b + 1) * P], y[:, b * P:(b + 1) * P], ident[:, :])
                last.then_inc(f_ty, 1)

            def chunk(c, first=False, last=False):
                if not last:
                    f_transpose_x(c + 1)
                if not first:
                    f_transpose_y(c - 1)
                for k in range(HCHUNKS):
                    f_down(c, k)
                    if not last:
                        f_hidden(c + 1, k)

            f_transpose_x(0)
            for k in range(HCHUNKS):
                f_hidden(0, k)
            chunk(0, first=True)
            chunk(1)
            with pe.Fori(2, GROUPS - 1) as c:
                chunk(c)
            chunk(GROUPS - 1, last=True)
            f_transpose_y(GROUPS - 1)

        @block.scalar
        def _(act):
            def identity(dst, src, col, rows=slice(0, P)):
                return act.activation(dst, src, ACT.Identity, bias=bias[rows, col:col + 1])

            def exponentials(g, s, first):
                act.wait_ge(neg_ready, g + 1)
                if not (first and s < 4):
                    act.wait_ge(t_done, g * 2 - 6)
                for hd in range(2):
                    for i in range(2):
                        n = 2 * hd + i
                        last = act.activation(probs[:, s % 4, hd, SEQ * i:SEQ * i + KEYS[i]],
                                              s_ps[2 * (s % 2) + hd][:, S_OFF[i]:S_OFF[i] + KEYS[i]],
                                              ACT.Exp, bias=neg_max[:, s % 4, n:n + 1], scale=SCALE,
                                              accum_out=row_sum[:, s % 4, n:n + 1])
                last.then_inc(exp_done, 1)

            def evacuate(task):
                kind, it, i = task
                if kind == "q":
                    act.wait_ge(q_done, it * 8 + i + 1)
                    identity(q_hi[:, i % 2, :], misc[:, :], B_QKV + i).then_inc(q_hi_ready, 1)
                elif kind == "k":
                    act.wait_ge(k_done, it * 8 + i + 1)
                    for hd in range(2):
                        rows = slice(hd * HEAD_DIM, (hd + 1) * HEAD_DIM)
                        identity(k_hi[rows, i % 2, hd, :], misc[rows, :], B_QKV + PAIRS + i, rows).then_inc(
                            k_hi_ready, 1)
                elif kind == "v":
                    act.wait_ge(v_done, it * 8 + i + 1)
                    act.copy(v[:, i % 4, i // 4 * 512:i // 4 * 512 + 512], misc[:, :]).then_inc(v_ready, 1)
                elif kind == "tx":
                    act.wait_ge(tx_done, it + 1)
                    act.copy(xnt_hi[:, :], misc[:, :]).then_inc(xnt_hi_ready, 1)
                elif kind == "m1":
                    act.wait_ge(m1_done, it + 1)
                    act.activation(e1[:, :], misc[:, :], ACT.Exp, bias=neg_b1[:, 0:1], scale=-1.0).then_inc(
                        e1_ready, 1)
                elif kind == "m2":
                    act.wait_ge(m2_done, it + 1)
                    identity(h_hi[:, :], misc[:, :], B_2).then_inc(h_hi_ready, 1)
                elif kind == "om":
                    act.wait_ge(om_done, it + 1)
                    identity(y[:, :], misc[:, :], B_O).then_inc(y_ready, 1)

            def probs_t_out(g, s, first):
                act.wait_ge(t_done, g * 2 + 1)
                if not (first and s < 2):
                    act.wait_ge(pv_done, g - 1)
                act.copy(probs_t[:, s % 2, 0, PT_FROM:], t_ps[0][:, PT_FROM:]).then_inc(pt_ready[0], 1)

            def values_out(g, s):
                act.wait_ge(pv_done, g + 1)
                p, b = s // 2, s % 2
                identity(o_hi[:, p, b * SEQ:(b + 1) * SEQ], pv_ps[:, 0:SEQ], B_QKV + 2 * PAIRS + p).then_inc(
                    o_hi_ready, 1)

            def group(it, first=False, last=False):
                for s in range(SLOTS):
                    g = it * SLOTS + s
                    if not (first and s == 0):
                        exponentials(g - 1, (s - 1) % SLOTS, first)
                    kind, ahead, i = task_a(s)
                    if not (last and ahead):
                        evacuate((kind, it + ahead, i))
                    if not (first and s < 2):
                        probs_t_out(g - 2, (s - 2) % SLOTS, first)
                    b_task = TASK_B.get(s)
                    if present(b_task, first, last) and b_task[0] == "om":
                        evacuate((b_task[0], it + b_task[1], b_task[2]))
                    if not (first and s < 3):
                        values_out(g - 3, (s - 3) % SLOTS)
                    if present(b_task, first, last) and b_task[0] != "om":
                        evacuate((b_task[0], it + b_task[1], b_task[2]))

            act.wait_ge(bias_in, 16)
            evacuate(("tx", 0, 0))
            act.wait_ge(w_ready, 1)
            evacuate(("m1", 0, 0))
            evacuate(("m2", 0, 0))
            evacuate(("q", 0, 0))
            evacuate(("k", 0, 0))
            evacuate(("v", 0, 0))
            evacuate(("v", 0, 1))
            act.wait_ge(zeros_ready, 1)
            group(0, first=True)
            with act.Fori(1, GROUPS - 1) as it:
                group(it)
            group(GROUPS - 1, last=True)
            n = GROUPS * SLOTS
            exponentials(n - 1, SLOTS - 1, False)
            for k in (2, 1):
                probs_t_out(n - k, SLOTS - k, False)
                values_out(n - k - 1, SLOTS - k - 1)
            values_out(n - 1, SLOTS - 1)
            evacuate(("om", GROUPS - 1, 0))

            def f_xnt_out(c):
                act.wait_ge(f_tx, c + 1)
                act.copy(xnt_hi[:, :], bank[0][:, :]).then_inc(f_xnt_hi, 1)

            def f_gelu_out(c, k):
                n = c * HCHUNKS + k
                act.wait_ge(f_m1, n + 1)
                if not (isinstance(n, int) and n < 2):
                    act.wait_ge(f_g, n - 1)
                act.activation(g_f32[k % 2][:, :], bank[1 + k][:, :], ACT.Gelu,
                               bias=bias[:, B_F1 + k:B_F1 + k + 1]).then_inc(f_gelu, 1)
                act.wait_ge(f_gelu, n + 1)
                act.copy(o_hi[:, k, :], g_f32[k % 2][:, :]).then_inc(f_g_hi, 1)

            def f_y_out(c):
                act.wait_ge(f_m2, c + 1)
                identity(y[:, :], bank[5][:, :], B_F2).then_inc(f_y, 1)

            f_xnt_out(0)
            for k in range(HCHUNKS):
                f_gelu_out(0, k)
            with act.Fori(0, GROUPS - 1) as c:
                f_xnt_out(c + 1)
                for k in range(HCHUNKS):
                    f_gelu_out(c + 1, k)
                f_y_out(c)
            f_y_out(GROUPS - 1)

        @block.vector
        def _(dve):
            def low(dst, src, hi, col=None, rows=slice(0, P)):
                if col is None:
                    return dve.tensor_tensor(dst, src, hi.bitcast(F32), ALU.subtract)
                return dve.scalar_tensor_tensor(out=dst, in0=src, scalar=bias[rows, col:col + 1],
                                                in1=hi.bitcast(F32), op0=ALU.add, op1=ALU.subtract)

            def moments(it, n, step, ready):
                for b in range(BLOCKS):
                    last = dve.bn_stats(stats[:, b, :], x_block(it, b))
                last.then_inc(step, 1)
                dve.wait_ge(step, n + 1)
                dve.sem_inc(dve_passed, 1)
                for b in range(BLOCKS):
                    last = dve.bn_aggr(mean_var[:, b, :], stats[:, b, :])
                last.then_inc(ready, 1)

            def normal_x(it, n, rstd_done, ready):
                dve.wait_ge(rstd_done, n + 1)
                for b in range(BLOCKS):
                    last = dve.tensor_scalar(xn[:, b, :], x_block(it, b), mean_var[:, b, 0:1],
                                             rstd[:, b:b + 1], ALU.subtract, ALU.mult)
                last.then_inc(ready, 1)

            def row_maxima(g, s):
                for hd in range(2):
                    dve.wait_ge(s_done, g * 2 + hd + 1)
                    dve.sem_inc(dve_passed, 1)
                    for i in range(2):
                        a = s_ps[2 * (s % 2) + hd][:, S_OFF[i]:S_OFF[i] + KEYS[i]]
                        last = dve.tensor_tensor_reduce(
                            out=a, in0=a, in1=mask[:, S_OFF[i]:S_OFF[i] + KEYS[i]], scale=1.0,
                            scalar=MASKED, op0=ALU.add, op1=ALU.max,
                            accum_out=row_max[:, s % 4, 2 * hd + i:2 * hd + i + 1])
                last.then_inc(max_done, 1)
                dve.wait_ge(max_done, g + 1)
                dve.tensor_scalar(neg_max[:, s % 4, :], row_max[:, s % 4, :], -SCALE, None,
                                  ALU.mult).then_inc(neg_ready, 1)

            def reciprocals(g, s):
                dve.wait_ge(exp_done, g + 1)
                dve.reciprocal(inv_sum[:, s % 4, :], row_sum[:, s % 4, :]).then_inc(inv_ready, 1)

            def evacuate(task):
                kind, it, i = task
                if kind == "q":
                    dve.wait_ge(q_hi_ready, it * 8 + i + 1)
                    low(q_lo[:, i % 2, :], misc[:, :], q_hi[:, i % 2, :], B_QKV + i).then_inc(q_ready, 1)
                elif kind == "k":
                    for hd in range(2):
                        dve.wait_ge(k_hi_ready, it * 16 + 2 * i + hd + 1)
                        rows = slice(hd * HEAD_DIM, (hd + 1) * HEAD_DIM)
                        last = low(k_lo[rows, i % 2, hd, :], misc[rows, :], k_hi[rows, i % 2, hd, :],
                                   B_QKV + PAIRS + i, rows)
                    last.then_inc(k_ready, 1)
                elif kind == "tx":
                    dve.wait_ge(xnt_hi_ready, it + 1)
                    low(xnt_lo[:, :], misc[:, :], xnt_hi[:, :]).then_inc(xnt_ready, 1)
                elif kind == "m1":
                    dve.wait_ge(e1_ready, it + 1)
                    dve.tensor_scalar(z1[:, :], misc[:, :], bias[:, B_1:B_1 + 1], None, ALU.add)
                    dve.tensor_scalar(e1[:, :], e1[:, :], 1.0, None, ALU.add).then_inc(silu_step, 1)
                    dve.wait_ge(silu_step, it * 4 + 1)
                    dve.reciprocal(e1[:, :], e1[:, :]).then_inc(silu_step, 1)
                    dve.wait_ge(silu_step, it * 4 + 2)
                    dve.tensor_tensor(z1[:, :], z1[:, :], e1[:, :], ALU.mult).then_inc(silu_step, 1)
                    dve.wait_ge(silu_step, it * 4 + 3)
                    dve.tensor_copy(s_hi[:, :], z1[:, :]).then_inc(silu_step, 1)
                    dve.wait_ge(silu_step, it * 4 + 4)
                    low(s_lo[:, :], z1[:, :], s_hi[:, :]).then_inc(s_ready, 1)
                elif kind == "m2":
                    dve.wait_ge(h_hi_ready, it + 1)
                    low(h_lo[:, :], misc[:, :], h_hi[:, :], B_2).then_inc(h_ready, 1)
                elif kind == "ty":
                    dve.wait_ge(ty_done, it + 1)
                    dve.tensor_tensor(x_group(it), misc[:, :], x_group(it), ALU.add).then_inc(x1_ready, 1)

            def probs_t_out(g, s, first):
                dve.wait_ge(t_done, g * 2 + 2)
                if not (first and s < 2):
                    dve.wait_ge(pv_done, g - 1)
                dve.tensor_copy(probs_t[:, s % 2, 1, PT_FROM:], t_ps[1][:, PT_FROM:]).then_inc(pt_ready[1], 1)

            def values_out(g, s):
                dve.wait_ge(o_hi_ready, g + 1)
                p, b = s // 2, s % 2
                low(o_lo[:, p, b * SEQ:(b + 1) * SEQ], pv_ps[:, 0:SEQ], o_hi[:, p, b * SEQ:(b + 1) * SEQ],
                    B_QKV + 2 * PAIRS + p).then_inc(o_ready, 1)

            def group(it, first=False, last=False):
                for s in range(SLOTS):
                    g = it * SLOTS + s
                    row_maxima(g, s)
                    if not (first and s == 0):
                        reciprocals(g - 1, (s - 1) % SLOTS)
                    kind, ahead, i = task_a(s)
                    if not (last and ahead):
                        evacuate((kind, it + ahead, i))
                    if not (first and s < 2):
                        probs_t_out(g - 2, (s - 2) % SLOTS, first)
                    if not (first and s < 3):
                        values_out(g - 3, (s - 3) % SLOTS)
                    b_task = TASK_B.get(s)
                    if present(b_task, first, last):
                        evacuate((b_task[0], it + b_task[1], b_task[2]))
                    if s == 6 and not last:
                        if first:
                            dve.wait_ge(x_rest_in, 16)
                        moments(it + 1, it + 1, stats_done, mv_ready)
                    if s == 8 and not last:
                        normal_x(it + 1, it + 1, rstd_ready, xn_ready)

            def split_weights(a, b, n):
                dve.tensor_copy(w_hi[:, a:b], w_raw[:, a:b]).then_inc(w_hi_ready, 1)
                dve.wait_ge(w_hi_ready, n)
                low(w_lo[:, a:b], w_raw[:, a:b], w_hi[:, a:b]).then_inc(w_ready, 1)

            dve.wait_ge(x_in, 16)
            moments(0, 0, stats_done, mv_ready)
            normal_x(0, 0, rstd_ready, xn_ready)
            dve.wait_ge(bias_in, 16)
            dve.tensor_scalar(neg_b1[:, :], bias[:, B_1:B_1 + 1], -1.0, None, ALU.mult)
            dve.wait_ge(w12_in, 32)
            split_weights(W_1, W_G, 1)
            evacuate(("tx", 0, 0))
            dve.wait_ge(wg_in, 16)
            split_weights(W_G, W_O, 2)
            evacuate(("m1", 0, 0))
            evacuate(("m2", 0, 0))
            evacuate(("q", 0, 0))
            evacuate(("k", 0, 0))
            dve.wait_ge(wof_in, 48)
            split_weights(W_O, N_W, 3)
            for part in (k_hi, k_lo):
                dve.memset(part[HEAD_DIM:P, :, 0, :].bitcast(F32), 0.0)
                dve.memset(part[0:HEAD_DIM, :, 1, :].bitcast(F32), 0.0)
            dve.wait_ge(w_ready, 3)
            dve.memset(probs[:, :, :, KEYS[0]:SEQ], 0.0).then_inc(zeros_ready, 1)
            dve.wait_ge(consts_ready, 2)
            group(0, first=True)
            with dve.Fori(1, GROUPS - 1) as it:
                group(it)
            group(GROUPS - 1, last=True)
            n = GROUPS * SLOTS
            reciprocals(n - 1, SLOTS - 1)
            for k in (2, 1):
                probs_t_out(n - k, SLOTS - k, False)
                values_out(n - k - 1, SLOTS - k - 1)
            values_out(n - 1, SLOTS - 1)
            evacuate(("ty", GROUPS - 1, 0))
            dve.wait_ge(x1_ready, GROUPS)

            def f_xnt_out(c):
                dve.wait_ge(f_xnt_hi, c + 1)
                low(xnt_lo[:, :], bank[0][:, :], xnt_hi[:, :]).then_inc(f_xnt, 1)

            def f_g_out(c, k):
                n = c * HCHUNKS + k
                dve.wait_ge(f_g_hi, n + 1)
                low(o_lo[:, k, :], g_f32[k % 2][:, :], o_hi[:, k, :]).then_inc(f_g, 1)

            def f_residual(c):
                dve.wait_ge(f_ty, c + 1)
                dve.tensor_tensor(x_group(c), bank[6][:, :], x_group(c), ALU.add).then_inc(f_out, 1)

            def f_moments(c):
                moments(c, c, f_stats, f_mv)

            f_moments(0)
            normal_x(0, 0, f_rstd, f_xn)
            dve.wait_ge(f_xn, 1)
            f_moments(1)
            f_xnt_out(0)
            normal_x(1, 1, f_rstd, f_xn)
            for k in range(HCHUNKS):
                f_g_out(0, k)

            def chunk(c, first=False, stats_ahead=True):
                f_xnt_out(c + 1)
                if not first:
                    f_residual(c - 1)
                f_g_out(c + 1, 0)
                if stats_ahead:
                    dve.wait_ge(f_xn, c + 2)
                    f_moments(c + 2)
                f_g_out(c + 1, 1)
                if stats_ahead:
                    normal_x(c + 2, c + 2, f_rstd, f_xn)
                for k in range(2, HCHUNKS):
                    f_g_out(c + 1, k)

            chunk(0, first=True)
            with dve.Fori(1, GROUPS - 2) as c:
                chunk(c)
            chunk(GROUPS - 2, stats_ahead=False)
            f_residual(GROUPS - 2)
            f_residual(GROUPS - 1)


def kernel(**inputs):
    import numpy as _np
    import concourse.bacc as _bacc
    from concourse import mybir as _mybir
    from concourse.bass_utils import run_bass_kernel_spmd as _run

    a = {k: _np.asarray(t) for k, t in inputs.items()}
    n, dim = BATCH * SEQ, DIM

    def columns(t):
        return t.reshape(-1, P).T

    arrays = {
        "x": a["L0_attn_x"].reshape(n, dim),
        "w1t": a["L0_attn_W1"].T,
        "w2t": a["L0_attn_W2"].T,
        "wgt": a["L0_attn_Wg"].T,
        "wot": a["L0_attn_Wo"].T.reshape(PAIRS, P, dim).transpose(1, 0, 2).reshape(P, PAIRS * dim),
        "fw1": a["L0_ffn_w1"],
        "fw2": a["L0_ffn_w2"].reshape(HCHUNKS, P, dim).transpose(1, 0, 2).reshape(P, HCHUNKS * dim),
        "biases": _np.concatenate([columns(a[k]) for k in (
            "L0_attn_bg", "L0_attn_b1", "L0_attn_b2", "L0_attn_bo", "L0_ffn_b1", "L0_ffn_b2")], axis=1),
    }
    arrays = {k: _np.ascontiguousarray(t) for k, t in arrays.items()}
    nc = _bacc.Bacc("TRN2", target_bir_lowering=False, num_devices=1)
    args = [nc.dram_tensor(f"in_{k}", t.shape, _mybir.dt.from_np(t.dtype), kind="ExternalInput").ap()
            for k, t in arrays.items()]
    out = nc.dram_tensor("out_0", (n, dim), F32, kind="ExternalOutput").ap()
    preln_block(nc, *args, out)
    r = _run(nc, [{f"in_{k}": t for k, t in arrays.items()}], core_ids=[0])
    return r.results[0]["out_0"].reshape(BATCH, SEQ, DIM)
```

```python
from contextlib import ExitStack

import concourse.bass as bass
from concourse import mybir

F32 = mybir.dt.float32
F32R = mybir.dt.float32r
ACT = mybir.ActivationFunctionType
ALU = mybir.AluOpType

P = 128
BATCH, SEQ, DIM = 32, 256, 128
HEADS, HEAD_DIM, WINDOW = 16, 64, 64
HIDDEN = 512
PAIRS = HEADS // 2
GROUP = 2 * SEQ
BLOCKS = GROUP // P
GROUPS = BATCH * SEQ // GROUP
SLOTS = 2 * PAIRS
HCHUNKS = HIDDEN // P
SCALE = HEAD_DIM ** -0.5
EPS = 1e-5
MASKED = -3.0e38

KEYS = [min(SEQ, P * (i + 1) + WINDOW) for i in range(2)]
M_OFF = [0, KEYS[0]]
PT_FROM = P - WINDOW

B_QKV, B_1, B_2, B_O, B_F1, B_F2 = 0, 24, 25, 26, 27, 31
N_BIAS = 32
W_1, W_2, W_G, W_V, W_O, W_F1, W_F2 = 0, 128, 256, 2304, 3328, 4352, 4864
N_W = 5376


def preln_block(nc, x, w1t, w2t, wgt, wot, fw1, fw2, biases, out):
    ctx = ExitStack()
    with ctx:
        def sb(name, shape, dt=F32):
            return ctx.enter_context(nc.sbuf_tensor(name, shape, dt))

        def sem(name):
            return ctx.enter_context(nc.semaphore(name))

        x_all = sb("x_all", [P, GROUPS * BLOCKS * DIM])
        bias = sb("bias", [P, N_BIAS])
        neg_b1 = sb("neg_b1", [P, 1])
        w_hi = sb("w_hi", [P, N_W], F32R)
        w_lo = sb("w_lo", [P, N_W], F32R)
        work = sb("work", [P, 12 * 512])
        w_raw = work[:, 0:W_O]
        late_raw = sb("late_raw", [P, N_W - W_O])
        probs = work[:, 0:8 * 512].rearrange("p (r h c) -> p r h c", r=4, h=2)
        probs_t = work[:, 8 * 512:12 * 512].rearrange("p (r h c) -> p r h c", r=2, h=2)
        ident = sb("ident", [P, P])
        mask = sb("mask", [P, sum(KEYS)])
        stats = sb("stats", [P, BLOCKS, 6])
        mean_var = sb("mean_var", [P, BLOCKS, 2])
        var_eps = sb("var_eps", [P, BLOCKS])
        rstd = sb("rstd", [P, BLOCKS])
        minus_half = sb("minus_half", [P, BLOCKS])
        xn = sb("xn", [P, BLOCKS, DIM])
        xnt_hi = sb("xnt_hi", [P, GROUP], F32R)
        xnt_lo = sb("xnt_lo", [P, GROUP], F32R)
        z1 = sb("z1", [P, GROUP])
        e1 = sb("e1", [P, GROUP])
        s_hi = sb("s_hi", [P, GROUP], F32R)
        s_lo = sb("s_lo", [P, GROUP], F32R)
        h_hi = sb("h_hi", [P, GROUP], F32R)
        h_lo = sb("h_lo", [P, GROUP], F32R)
        q_hi = sb("q_hi", [P, 2, GROUP], F32R)
        q_lo = sb("q_lo", [P, 2, GROUP], F32R)
        k_hi = sb("k_hi", [P, 2, 2, GROUP], F32R)
        k_lo = sb("k_lo", [P, 2, 2, GROUP], F32R)
        v = sb("v", [P, BLOCKS, HEADS * HEAD_DIM])
        o_f32 = sb("o_f32", [P, 2, SEQ])
        o_hi = sb("o_hi", [P, HCHUNKS, GROUP], F32R)
        o_lo = sb("o_lo", [P, HCHUNKS, GROUP], F32R)
        y = sb("y", [P, GROUP])
        row_max = sb("row_max", [P, 4, 4])
        neg_max = sb("neg_max", [P, 4, 4])
        row_sum = sb("row_sum", [P, 4, 4])
        inv_sum = sb("inv_sum", [P, 4, 4])
        g_f32 = [z1, e1]

        bank = [ctx.enter_context(nc.psum_tensor(f"bank{i}", [P, 512], F32)) for i in range(8)]
        s_ps = bank[0:2]
        t_ps = bank[2:4]
        pv_ps = bank[4]
        o_ps = bank[5]
        qk_ps = bank[6]
        misc = bank[7]

        x_in, x_rest_in, w12_in, wg_in, wof_in, bias_in = map(
            sem, ("x_in", "x_rest_in", "w12_in", "wg_in", "wof_in", "bias_in"))
        consts_ready = sem("consts_ready")
        zeros_ready = sem("zeros_ready")
        w12_hi_ready, w12_ready = sem("w12_hi_ready"), sem("w12_ready")
        wg_hi_ready, wg_ready = sem("wg_hi_ready"), sem("wg_ready")
        wof_hi_ready, wof_ready = sem("wof_hi_ready"), sem("wof_ready")
        stats_done, mv_ready = sem("stats_done"), sem("mv_ready")
        rstd_step, rstd_ready, xn_ready = sem("rstd_step"), sem("rstd_ready"), sem("xn_ready")
        tx_done, xnt_hi_ready, xnt_ready = sem("tx_done"), sem("xnt_hi_ready"), sem("xnt_ready")
        m1_done, e1_ready, z1_ready = sem("m1_done"), sem("e1_ready"), sem("z1_ready")
        silu_step, s_ready = sem("silu_step"), sem("s_ready")
        m2_done, h_hi_ready, h_ready = sem("m2_done"), sem("h_hi_ready"), sem("h_ready")
        q_done, q_hi_ready, q_ready = sem("q_done"), sem("q_hi_ready"), sem("q_ready")
        k_done, k_hi_ready, k_ready = sem("k_done"), sem("k_hi_ready"), sem("k_ready")
        v_done, v_ready = sem("v_done"), sem("v_ready")
        s_done = sem("s_done")
        max_done, neg_ready = sem("max_done"), sem("neg_ready")
        exp_done, inv_ready, norm_done = sem("exp_done"), sem("inv_ready"), sem("norm_done")
        t_done = sem("t_done")
        pt_ready = [sem("pt0_ready"), sem("pt1_ready")]
        pv_done, o_hi_ready, o_ready = sem("pv_done"), sem("o_hi_ready"), sem("o_ready")
        o_f32_ready = sem("o_f32_ready")
        om_done, y_ready, ty_done, x1_ready = sem("om_done"), sem("y_ready"), sem("ty_done"), sem("x1_ready")
        f_stats, f_mv, f_rstd_step = sem("f_stats"), sem("f_mv"), sem("f_rstd_step")
        f_rstd, f_xn = sem("f_rstd"), sem("f_xn")
        f_tx, f_xnt_hi, f_xnt = sem("f_tx"), sem("f_xnt_hi"), sem("f_xnt")
        f_m1, f_gelu_done, f_g_hi, f_g = sem("f_m1"), sem("f_gelu_done"), sem("f_g_hi"), sem("f_g")
        f_g_pool_hi, f_g_pool = sem("f_g_pool_hi"), sem("f_g_pool")
        f_m2, f_y, f_ty, f_out = sem("f_m2"), sem("f_y"), sem("f_ty"), sem("f_out")
        stored = sem("stored")
        dve_passed, pool_passed = sem("dve_passed"), sem("pool_passed")

        def split_product(eng, out_ap, w, a, first=True, last=True):
            eng.matmul(out_ap, w[0], a[0], start=first, stop=False)
            eng.matmul(out_ap, w[0], a[1], start=False, stop=False)
            return eng.matmul(out_ap, w[1], a[0], start=False, stop=last)

        def w_parts(at, n=P):
            return w_hi[:, at:at + n], w_lo[:, at:at + n]

        def x_group(it):
            return x_all[:, bass.ds(it * (BLOCKS * DIM), BLOCKS * DIM)]

        def x_block(it, b):
            return x_all[:, bass.ds(it * (BLOCKS * DIM) + b * DIM, DIM)]

        x_v = x.rearrange("(n p) d -> p n d", p=P)
        out_v = out.rearrange("(n p) d -> p n d", p=P)
        block = ctx.enter_context(nc.Block())

        def task_a(s):
            kind, pair = ("q", (s + 3) // 2) if s % 2 else ("k", (s + 2) // 2)
            return kind, pair // PAIRS, pair % PAIRS

        TASK_B = {0: ("v", 0, 2), 1: ("v", 0, 3), 2: ("v", 0, 4), 3: ("v", 0, 5), 4: ("v", 0, 6),
                  5: ("v", 0, 7), 6: ("tx", 1, 0), 7: ("m1", 1, 0), 8: ("ty", -1, 0),
                  12: ("m2", 1, 0), 14: ("v", 1, 0), 15: ("v", 1, 1)}

        def out_pair(s):
            if s % 2 == 0:
                return None
            pair = (s - 7) // 2
            return (0, pair) if pair >= 0 else (-1, pair + PAIRS)

        MOMENTS_AT, DEVIATIONS_AT, NORMAL_AT = 3, 4, 5
        SILU_AT = {8: (0,), 9: (1,), 10: (2, 3)}
        SILU_START, SILU_PRODUCT, SILU_PARTS = 7, 11, 12

        def present(task, first, last):
            return task is not None and not (first and task[1] < 0) and not (last and task[1] > 0)

        @block.sync
        def _(sp):
            sp.dma_start(x_all[:, 0:BLOCKS * DIM].rearrange("p (n d) -> p n d", d=DIM),
                         x_v[:, 0:BLOCKS, :]).then_inc(x_in, 16)
            sp.dma_start(w_raw[:, W_1:W_1 + P], w1t).then_inc(w12_in, 16)
            sp.dma_start(w_raw[:, W_2:W_2 + P], w2t).then_inc(w12_in, 16)
            sp.dma_start(bias[:, :], biases).then_inc(bias_in, 16)
            sp.dma_start(w_raw[:, W_G:W_O], wgt).then_inc(wg_in, 16)
            sp.dma_start(late_raw[:, 0:W_F1 - W_O], wot).then_inc(wof_in, 16)
            sp.dma_start(late_raw[:, W_F1 - W_O:W_F2 - W_O], fw1).then_inc(wof_in, 16)
            sp.dma_start(late_raw[:, W_F2 - W_O:N_W - W_O], fw2).then_inc(wof_in, 16)
            sp.dma_start(x_all[:, BLOCKS * DIM:].rearrange("p (n d) -> p n d", d=DIM),
                         x_v[:, BLOCKS:, :]).then_inc(x_rest_in, 16)

            def store(c):
                sp.wait_ge(f_out, c + 1)
                sp.dma_start(out_v[:, bass.ds(c * BLOCKS, BLOCKS), :],
                             x_group(c).rearrange("p (n d) -> p n d", d=DIM)).then_inc(stored, 16)

            with sp.Fori(0, GROUPS) as c:
                store(c)
            sp.wait_ge(stored, 16 * GROUPS)

        @block.gpsimd
        def _(pool):
            pool.memset(ident[:, :], 0.0)
            pool.memset(minus_half[:, :], -0.5)
            pool.memset(mask[:, :], 0.0).then_inc(consts_ready, 1)
            pool.wait_ge(consts_ready, 1)
            pool.affine_select(out=ident[:, :], in_=ident[:, :], compare_op=ALU.not_equal, fill=1.0,
                               base=0, pattern=[[-1, P]], channel_multiplier=1)
            for i in range(2):
                m = mask[:, M_OFF[i]:M_OFF[i] + KEYS[i]]
                last = pool.affine_select(out=m, in_=m, compare_op=ALU.is_ge, fill=MASKED,
                                          base=P * i + WINDOW - 1, pattern=[[-1, KEYS[i]]],
                                          channel_multiplier=1)
            last.then_inc(consts_ready, 1)

            def inverse_deviations(n, moments, step, ready):
                pool.wait_ge(moments, n + 1)
                pool.sem_inc(pool_passed, 1)
                pool.tensor_scalar(var_eps[:, :], mean_var[:, :, 1], EPS, 1.0, ALU.add,
                                   ALU.mult).then_inc(step, 1)
                pool.wait_ge(step, n + 1)
                pool.tensor_tensor(rstd[:, :], var_eps[:, :], minus_half[:, :], ALU.pow).then_inc(ready, 1)

            def normalise(g, s):
                pool.wait_ge(inv_ready, g + 1)
                pool.sem_inc(pool_passed, 1)
                for hd in range(2):
                    for i in range(2):
                        a = probs[:, s % 4, hd, SEQ * i:SEQ * i + KEYS[i]]
                        last = pool.tensor_scalar(a, a, inv_sum[:, s % 4, 2 * hd + i:2 * hd + i + 1], 1.0,
                                                  ALU.mult, ALU.mult)
                last.then_inc(norm_done, 1)

            def values_parts(g, s):
                p, cols = s // 2 % 2, slice(s % 2 * SEQ, s % 2 * SEQ + SEQ)
                pool.wait_ge(o_f32_ready, g + 1)
                pool.sem_inc(pool_passed, 1)
                pool.tensor_scalar(o_hi[:, p, cols], o_f32[:, s % 2, :], 1.0, 1.0, ALU.mult,
                                   ALU.mult).then_inc(o_hi_ready, 1)
                pool.wait_ge(o_hi_ready, g + 1)
                pool.tensor_tensor(o_lo[:, p, cols], o_f32[:, s % 2, :], o_hi[:, p, cols].bitcast(F32),
                                   ALU.subtract).then_inc(o_ready, 1)

            def silu_product(it):
                pool.wait_ge(silu_step, it * 4 + 2)
                pool.tensor_tensor(z1[:, :], z1[:, :], e1[:, :], ALU.mult).then_inc(silu_step, 1)

            def silu_parts(it):
                pool.wait_ge(silu_step, it * 4 + 3)
                pool.sem_inc(pool_passed, 1)
                pool.tensor_scalar(s_hi[:, :], z1[:, :], 1.0, 1.0, ALU.mult, ALU.mult).then_inc(silu_step, 1)
                pool.wait_ge(silu_step, it * 4 + 4)
                pool.tensor_tensor(s_lo[:, :], z1[:, :], s_hi[:, :].bitcast(F32),
                                   ALU.subtract).then_inc(s_ready, 1)

            def group(it, first=False, last=False):
                for s in range(SLOTS):
                    if s == SILU_PRODUCT and not last:
                        silu_product(it + 1)
                    if s == SILU_PARTS and not last:
                        silu_parts(it + 1)
                    if not (first and s < 4):
                        values_parts(it * SLOTS + s - 4, (s - 4) % SLOTS)
                    if not (first and s == 0):
                        normalise(it * SLOTS + s - 1, (s - 1) % SLOTS)
                    if s == DEVIATIONS_AT and not last:
                        inverse_deviations(it + 1, mv_ready, rstd_step, rstd_ready)

            inverse_deviations(0, mv_ready, rstd_step, rstd_ready)
            pool.memset(k_hi[:, :, :, :].bitcast(F32), 0.0)
            pool.memset(k_lo[:, :, :, :].bitcast(F32), 0.0).then_inc(zeros_ready, 1)
            for n, (a, b) in enumerate(((W_G, W_V), (W_V, W_O))):
                if n == 1:
                    silu_product(0)
                    silu_parts(0)
                pool.wait_ge(wg_hi_ready, n + 1)
                pool.tensor_tensor(w_lo[:, a:b], w_raw[:, a:b], w_hi[:, a:b].bitcast(F32),
                                   ALU.subtract).then_inc(wg_ready, 1)
            pool.wait_ge(wg_ready, 2)
            pool.wait_ge(w12_ready, 1)
            pool.memset(probs[:, :, :, KEYS[0]:SEQ], 0.0).then_inc(zeros_ready, 1)
            pool.wait_ge(wof_in, 48)
            pool.tensor_scalar(w_hi[:, W_O:N_W], late_raw[:, :], 1.0, 1.0, ALU.mult,
                               ALU.mult).then_inc(wof_hi_ready, 1)
            pool.wait_ge(wof_hi_ready, 1)
            pool.tensor_tensor(w_lo[:, W_O:N_W], late_raw[:, :], w_hi[:, W_O:N_W].bitcast(F32),
                               ALU.subtract).then_inc(wof_ready, 1)
            group(0, first=True)
            with pool.Fori(1, GROUPS - 1) as it:
                group(it)
            group(GROUPS - 1, last=True)
            n = GROUPS * SLOTS
            values_parts(n - 4, SLOTS - 4)
            normalise(n - 1, SLOTS - 1)
            for k in (3, 2, 1):
                values_parts(n - k, SLOTS - k)

            def f_g_parts(c):
                k = HCHUNKS - 1
                pool.wait_ge(f_gelu_done, (c + 1) * HCHUNKS)
                pool.sem_inc(pool_passed, 1)
                pool.tensor_scalar(o_hi[:, k, :], g_f32[k % 2][:, :], 1.0, 1.0, ALU.mult,
                                   ALU.mult).then_inc(f_g_pool_hi, 1)
                pool.wait_ge(f_g_pool_hi, c + 1)
                pool.tensor_tensor(o_lo[:, k, :], g_f32[k % 2][:, :], o_hi[:, k, :].bitcast(F32),
                                   ALU.subtract).then_inc(f_g_pool, 1)

            inverse_deviations(0, f_mv, f_rstd_step, f_rstd)
            inverse_deviations(1, f_mv, f_rstd_step, f_rstd)
            f_g_parts(0)
            with pool.Fori(2, GROUPS) as c:
                inverse_deviations(c, f_mv, f_rstd_step, f_rstd)
                f_g_parts(c - 1)
            f_g_parts(GROUPS - 1)

        @block.tensor
        def _(pe):
            def free(task):
                kind, it, i = task
                if kind in "qkv":
                    pe.wait_ge({"q": q_ready, "k": k_ready, "v": v_ready}[kind], it * 8 + i + 1)
                else:
                    pe.wait_ge({"tx": xnt_ready, "m1": z1_ready, "m2": h_ready,
                                "ty": x1_ready}[kind], it + 1)

            def do(task):
                kind, it, i = task
                if kind == "tx":
                    pe.wait_ge(xn_ready, it + 1)
                    for b in range(BLOCKS):
                        last = pe.transpose(misc[:, b * P:(b + 1) * P], xn[:, b, :], ident[:, :])
                    last.then_inc(tx_done, 1)
                elif kind == "m1":
                    pe.wait_ge(xnt_ready, it + 1)
                    split_product(pe, misc[:, :], w_parts(W_1), (xnt_hi[:, :], xnt_lo[:, :])).then_inc(m1_done, 1)
                elif kind == "m2":
                    pe.wait_ge(s_ready, it + 1)
                    split_product(pe, misc[:, :], w_parts(W_2), (s_hi[:, :], s_lo[:, :])).then_inc(m2_done, 1)
                elif kind in "qk":
                    pe.wait_ge(h_ready, it + 1)
                    at = W_G + (kind == "k") * HEADS * HEAD_DIM + i * P
                    split_product(pe, qk_ps[:, :], w_parts(at), (h_hi[:, :], h_lo[:, :])).then_inc(
                        q_done if kind == "q" else k_done, 1)
                elif kind == "v":
                    pe.wait_ge(h_ready, it + 1)
                    b, at = i % 4, W_V + i // 4 * 512
                    cols = slice(b * P, (b + 1) * P)
                    split_product(pe, misc[:, :], (h_hi[:, cols], h_lo[:, cols]),
                                  w_parts(at, 512)).then_inc(v_done, 1)
                elif kind == "ty":
                    pe.wait_ge(y_ready, it + 1)
                    for b in range(BLOCKS):
                        last = pe.transpose(misc[:, b * P:(b + 1) * P], y[:, b * P:(b + 1) * P], ident[:, :])
                    last.then_inc(ty_done, 1)

            def out_projection(it, p, first):
                pe.wait_ge(o_ready, it * SLOTS + 2 * p + 2)
                if p == 0 and not first:
                    pe.wait_ge(y_ready, it)
                last = split_product(pe, o_ps[:, :], w_parts(W_O + p * P),
                                     (o_hi[:, p % 2, :], o_lo[:, p % 2, :]), first=p == 0, last=p == PAIRS - 1)
                if p == PAIRS - 1:
                    last.then_inc(om_done, 1)

            def scores(it, s, first):
                g, p, b = it * SLOTS + s, s // 2, s % 2
                pe.wait_ge(q_ready, it * 8 + p + 1)
                pe.wait_ge(k_ready, it * 8 + p + 1)
                for i in range(2):
                    if not (first and s == 0):
                        pe.wait_ge(max_done, g * 2 - 1 + i)
                    dst = s_ps[i][:, 0:2 * KEYS[i]].rearrange("p (h c) -> p h c", h=2)
                    rows = slice(b * SEQ + i * P, b * SEQ + (i + 1) * P)
                    cols = slice(b * SEQ, b * SEQ + KEYS[i])
                    split_product(pe, dst, (q_hi[:, p % 2, rows], q_lo[:, p % 2, rows]),
                                  (k_hi[:, p % 2, :, cols], k_lo[:, p % 2, :, cols])).then_inc(s_done, 1)

            def transposes(it, s, first):
                g = it * SLOTS + s
                pe.wait_ge(norm_done, g + 1)
                for hd in range(2):
                    if not (first and s == 0):
                        pe.wait_ge(pt_ready[hd], g)
                    for n, j in enumerate((1, 0)):
                        for i in range(2):
                            last = pe.transpose(t_ps[hd][:, SEQ * n + P * i:SEQ * n + P * (i + 1)],
                                                probs[:, s % 4, hd, SEQ * i + P * j:SEQ * i + P * (j + 1)],
                                                ident[:, :])
                    last.then_inc(t_done, 1)

            def values(it, s, first):
                g, p, b = it * SLOTS + s, s // 2, s % 2
                for hd in range(2):
                    pe.wait_ge(pt_ready[hd], g + 1)
                pe.wait_ge(v_ready, it * 8 + p // 4 * 4 + 2 * b + 2)
                if not (first and s == 0):
                    pe.wait_ge(o_f32_ready, g)
                for j in range(2):
                    for hd in range(2):
                        head = (2 * p + hd) * HEAD_DIM
                        dst = pv_ps[hd * HEAD_DIM:(hd + 1) * HEAD_DIM, PT_FROM * j:SEQ]
                        src = probs_t[:, s % 2, hd, (SEQ, PT_FROM)[j]:(2 * SEQ, SEQ)[j]]
                        last = pe.matmul(dst, v[:, 2 * b + j, head:head + HEAD_DIM], src,
                                         start=j == 0, stop=j == 1)
                last.then_inc(pv_done, 1)

            def group(it, first=False, last=False):
                prev_a, prev = ("q", it, 1), ("v", it, 1)
                for s in range(SLOTS):
                    scores(it, s, first)
                    kind, ahead, i = task_a(s)
                    if not (last and ahead):
                        free(prev_a)
                        prev_a = (kind, it + ahead, i)
                        do(prev_a)
                    before, same = (it, True) if s >= 2 else (it - 1, False)
                    if same or not first:
                        transposes(before, (s - 2) % SLOTS, first and same)
                    if s == 7 and first:
                        pe.wait_ge(wof_ready, 1)
                    if out_pair(s) and not (first and out_pair(s)[0]):
                        out_projection(it + out_pair(s)[0], out_pair(s)[1], first)
                    before, same = (it, True) if s >= 3 else (it - 1, False)
                    if same or not first:
                        values(before, (s - 3) % SLOTS, first and same)
                    b_task = TASK_B.get(s)
                    if present(b_task, first, last):
                        free(prev)
                        prev = (b_task[0], it + b_task[1], b_task[2])
                        do(prev)
                return prev

            pe.wait_ge(consts_ready, 2)
            do(("tx", 0, 0))
            pe.wait_ge(w12_ready, 1)
            do(("m1", 0, 0))
            do(("m2", 0, 0))
            pe.wait_ge(wg_ready, 1)
            do(("q", 0, 0))
            free(("q", 0, 0))
            do(("k", 0, 0))
            pe.wait_ge(wg_ready, 2)
            do(("v", 0, 0))
            free(("k", 0, 0))
            do(("q", 0, 1))
            free(("v", 0, 0))
            do(("v", 0, 1))
            pe.wait_ge(zeros_ready, 1)
            group(0, first=True)
            with pe.Fori(1, GROUPS - 1) as it:
                group(it)
            end = GROUPS - 1
            prev = group(end, last=True)
            transposes(end, SLOTS - 2, False)
            values(end, SLOTS - 3, False)
            transposes(end, SLOTS - 1, False)
            out_projection(end, PAIRS - 3, False)
            values(end, SLOTS - 2, False)
            values(end, SLOTS - 1, False)
            out_projection(end, PAIRS - 2, False)
            out_projection(end, PAIRS - 1, False)
            free(prev)
            do(("ty", end, 0))
            free(("ty", end, 0))

            def f_transpose_x(c):
                pe.wait_ge(f_xn, c + 1)
                for b in range(BLOCKS):
                    last = pe.transpose(bank[0][:, b * P:(b + 1) * P], xn[:, b, :], ident[:, :])
                last.then_inc(f_tx, 1)

            def f_hidden(c, k):
                if k == 0:
                    pe.wait_ge(f_xnt, c + 1)
                split_product(pe, bank[1 + k][:, :], w_parts(W_F1 + k * P),
                              (xnt_hi[:, :], xnt_lo[:, :])).then_inc(f_m1, 1)

            def f_down(c, k):
                if k == HCHUNKS - 1:
                    pe.wait_ge(f_g_pool, c + 1)
                else:
                    pe.wait_ge(f_g, c * 3 + k + 1)
                last = split_product(pe, bank[5][:, :], w_parts(W_F2 + k * P), (o_hi[:, k, :], o_lo[:, k, :]),
                                     first=k == 0, last=k == HCHUNKS - 1)
                if k == HCHUNKS - 1:
                    last.then_inc(f_m2, 1)

            def f_transpose_y(c):
                pe.wait_ge(f_y, c + 1)
                if not (isinstance(c, int) and c < 1):
                    pe.wait_ge(f_out, c)
                for b in range(BLOCKS):
                    last = pe.transpose(bank[6][:, b * P:(b + 1) * P], y[:, b * P:(b + 1) * P], ident[:, :])
                last.then_inc(f_ty, 1)

            def chunk(c, first=False, last=False):
                if not last:
                    f_transpose_x(c + 1)
                if not first:
                    f_transpose_y(c - 1)
                for k in range(HCHUNKS):
                    f_down(c, k)
                    if not last:
                        f_hidden(c + 1, k)

            f_transpose_x(0)
            for k in range(HCHUNKS):
                f_hidden(0, k)
            chunk(0, first=True)
            chunk(1)
            with pe.Fori(2, GROUPS - 1) as c:
                chunk(c)
            chunk(GROUPS - 1, last=True)
            f_transpose_y(GROUPS - 1)

        @block.scalar
        def _(act):
            def identity(dst, src, col, rows=slice(0, P)):
                return act.activation(dst, src, ACT.Identity, bias=bias[rows, col:col + 1])

            def exponentials(g, s, first):
                act.wait_ge(neg_ready, g + 1)
                for hd in range(2):
                    for i in range(2):
                        n = 2 * hd + i
                        a = probs[:, s % 4, hd, SEQ * i:SEQ * i + KEYS[i]]
                        last = act.activation(a, a, ACT.Exp, bias=neg_max[:, s % 4, n:n + 1], scale=SCALE,
                                              accum_out=row_sum[:, s % 4, n:n + 1])
                last.then_inc(exp_done, 1)

            def evacuate(task):
                kind, it, i = task
                if kind == "q":
                    act.wait_ge(q_done, it * 8 + i + 1)
                    identity(q_hi[:, i % 2, :], qk_ps[:, :], B_QKV + i).then_inc(q_hi_ready, 1)
                elif kind == "k":
                    act.wait_ge(k_done, it * 8 + i + 1)
                    for hd in range(2):
                        rows = slice(hd * HEAD_DIM, (hd + 1) * HEAD_DIM)
                        identity(k_hi[rows, i % 2, hd, :], qk_ps[rows, :], B_QKV + PAIRS + i, rows).then_inc(
                            k_hi_ready, 1)
                elif kind == "v":
                    act.wait_ge(v_done, it * 8 + i + 1)
                    act.copy(v[:, i % 4, i // 4 * 512:i // 4 * 512 + 512], misc[:, :]).then_inc(v_ready, 1)
                elif kind == "tx":
                    act.wait_ge(tx_done, it + 1)
                    act.copy(xnt_hi[:, :], misc[:, :]).then_inc(xnt_hi_ready, 1)
                elif kind == "m1":
                    act.wait_ge(m1_done, it + 1)
                    act.activation(e1[:, :], misc[:, :], ACT.Exp, bias=neg_b1[:, 0:1], scale=-1.0).then_inc(
                        e1_ready, 1)
                elif kind == "m2":
                    act.wait_ge(m2_done, it + 1)
                    identity(h_hi[:, :], misc[:, :], B_2).then_inc(h_hi_ready, 1)

            def probs_t_out(g, s, first):
                act.wait_ge(t_done, g * 2 + 1)
                if not (first and s < 2):
                    act.wait_ge(pv_done, g - 1)
                act.copy(probs_t[:, s % 2, 0, PT_FROM:], t_ps[0][:, PT_FROM:]).then_inc(pt_ready[0], 1)

            def values_out(g, s, first):
                act.wait_ge(pv_done, g + 1)
                if not (first and s < 2):
                    act.wait_ge(o_ready, g - 1)
                identity(o_f32[:, s % 2, :], pv_ps[:, 0:SEQ], B_QKV + 2 * PAIRS + s // 2).then_inc(
                    o_f32_ready, 1)

            def projection_out(it):
                act.wait_ge(om_done, it + 1)
                identity(y[:, :], o_ps[:, :], B_O).then_inc(y_ready, 1)

            def group(it, first=False, last=False):
                for s in range(SLOTS):
                    g = it * SLOTS + s
                    if not (first and s == 0):
                        exponentials(g - 1, (s - 1) % SLOTS, first)
                    kind, ahead, i = task_a(s)
                    if not (last and ahead):
                        evacuate((kind, it + ahead, i))
                    if not (first and s < 2):
                        probs_t_out(g - 2, (s - 2) % SLOTS, first)
                    if s == 5 and not first:
                        projection_out(it - 1)
                    if not (first and s < 3):
                        values_out(g - 3, (s - 3) % SLOTS, first)
                    b_task = TASK_B.get(s)
                    if present(b_task, first, last):
                        evacuate((b_task[0], it + b_task[1], b_task[2]))

            act.wait_ge(bias_in, 16)
            evacuate(("tx", 0, 0))
            act.wait_ge(wg_in, 16)
            for a, b in ((W_G, W_V), (W_V, W_O)):
                act.copy(w_hi[:, a:b], w_raw[:, a:b]).then_inc(wg_hi_ready, 1)
            act.wait_ge(w12_ready, 1)
            evacuate(("m1", 0, 0))
            evacuate(("m2", 0, 0))
            evacuate(("q", 0, 0))
            act.wait_ge(zeros_ready, 1)
            evacuate(("k", 0, 0))
            evacuate(("v", 0, 0))
            evacuate(("q", 0, 1))
            evacuate(("v", 0, 1))
            group(0, first=True)
            with act.Fori(1, GROUPS - 1) as it:
                group(it)
            group(GROUPS - 1, last=True)
            n = GROUPS * SLOTS
            exponentials(n - 1, SLOTS - 1, False)
            for k in (2, 1):
                probs_t_out(n - k, SLOTS - k, False)
                values_out(n - k - 1, SLOTS - k - 1, False)
            values_out(n - 1, SLOTS - 1, False)
            projection_out(GROUPS - 1)

            def f_xnt_out(c):
                act.wait_ge(f_tx, c + 1)
                act.copy(xnt_hi[:, :], bank[0][:, :]).then_inc(f_xnt_hi, 1)

            def f_gelu(c, k):
                act.wait_ge(f_m1, c * HCHUNKS + k + 1)
                if not (isinstance(c, int) and c == 0):
                    if k == 1:
                        act.wait_ge(f_g_pool, c)
                if k >= 2:
                    act.wait_ge(f_g, c * 3 + k - 1)
                act.activation(g_f32[k % 2][:, :], bank[1 + k][:, :], ACT.Gelu,
                               bias=bias[:, B_F1 + k:B_F1 + k + 1]).then_inc(f_gelu_done, 1)

            def f_g_high(c, k):
                act.wait_ge(f_gelu_done, c * HCHUNKS + k + 1)
                act.copy(o_hi[:, k, :], g_f32[k % 2][:, :]).then_inc(f_g_hi, 1)

            def f_hidden_out(c):
                f_gelu(c, 0)
                f_gelu(c, 1)
                f_g_high(c, 0)
                f_g_high(c, 1)
                f_gelu(c, 2)
                f_gelu(c, 3)
                f_g_high(c, 2)

            def f_y_out(c):
                act.wait_ge(f_m2, c + 1)
                identity(y[:, :], bank[5][:, :], B_F2).then_inc(f_y, 1)

            f_xnt_out(0)
            f_hidden_out(0)
            with act.Fori(0, GROUPS - 1) as c:
                f_xnt_out(c + 1)
                f_hidden_out(c + 1)
                f_y_out(c)
            f_y_out(GROUPS - 1)

        @block.vector
        def _(dve):
            def low(dst, src, hi, col=None, rows=slice(0, P)):
                if col is None:
                    return dve.tensor_tensor(dst, src, hi.bitcast(F32), ALU.subtract)
                return dve.scalar_tensor_tensor(out=dst, in0=src, scalar=bias[rows, col:col + 1],
                                                in1=hi.bitcast(F32), op0=ALU.add, op1=ALU.subtract)

            def moments(it, n, step, ready):
                for b in range(BLOCKS):
                    last = dve.bn_stats(stats[:, b, :], x_block(it, b))
                last.then_inc(step, 1)
                dve.wait_ge(step, n + 1)
                dve.sem_inc(dve_passed, 1)
                for b in range(BLOCKS):
                    last = dve.bn_aggr(mean_var[:, b, :], stats[:, b, :])
                last.then_inc(ready, 1)

            def normal_x(it, n, rstd_done, ready):
                dve.wait_ge(rstd_done, n + 1)
                for b in range(BLOCKS):
                    last = dve.tensor_scalar(xn[:, b, :], x_block(it, b), mean_var[:, b, 0:1],
                                             rstd[:, b:b + 1], ALU.subtract, ALU.mult)
                last.then_inc(ready, 1)

            def row_maxima(g, s, first):
                if not (first and s < 4):
                    dve.wait_ge(t_done, g * 2 - 6)
                for i in range(2):
                    dve.wait_ge(s_done, g * 2 + i + 1)
                    dve.sem_inc(dve_passed, 1)
                    for hd in range(2):
                        last = dve.tensor_tensor_reduce(
                            out=probs[:, s % 4, hd, SEQ * i:SEQ * i + KEYS[i]],
                            in0=s_ps[i][:, hd * KEYS[i]:(hd + 1) * KEYS[i]], in1=mask[:, M_OFF[i]:M_OFF[i] + KEYS[i]], scale=1.0,
                            scalar=MASKED, op0=ALU.add, op1=ALU.max,
                            accum_out=row_max[:, s % 4, 2 * hd + i:2 * hd + i + 1])
                    last.then_inc(max_done, 1)
                dve.wait_ge(max_done, g * 2 + 2)
                dve.tensor_scalar(neg_max[:, s % 4, :], row_max[:, s % 4, :], -SCALE, None,
                                  ALU.mult).then_inc(neg_ready, 1)

            def reciprocals(g, s):
                dve.wait_ge(exp_done, g + 1)
                dve.reciprocal(inv_sum[:, s % 4, :], row_sum[:, s % 4, :]).then_inc(inv_ready, 1)

            def evacuate(task):
                kind, it, i = task
                if kind == "q":
                    dve.wait_ge(q_hi_ready, it * 8 + i + 1)
                    low(q_lo[:, i % 2, :], qk_ps[:, :], q_hi[:, i % 2, :], B_QKV + i).then_inc(q_ready, 1)
                elif kind == "k":
                    for hd in range(2):
                        dve.wait_ge(k_hi_ready, it * 16 + 2 * i + hd + 1)
                        rows = slice(hd * HEAD_DIM, (hd + 1) * HEAD_DIM)
                        last = low(k_lo[rows, i % 2, hd, :], qk_ps[rows, :], k_hi[rows, i % 2, hd, :],
                                   B_QKV + PAIRS + i, rows)
                    last.then_inc(k_ready, 1)
                elif kind == "tx":
                    dve.wait_ge(xnt_hi_ready, it + 1)
                    low(xnt_lo[:, :], misc[:, :], xnt_hi[:, :]).then_inc(xnt_ready, 1)
                elif kind == "m2":
                    dve.wait_ge(h_hi_ready, it + 1)
                    low(h_lo[:, :], misc[:, :], h_hi[:, :], B_2).then_inc(h_ready, 1)
                elif kind == "ty":
                    dve.wait_ge(ty_done, it + 1)
                    dve.tensor_tensor(x_group(it), misc[:, :], x_group(it), ALU.add).then_inc(x1_ready, 1)

            def silu_start(it):
                dve.wait_ge(e1_ready, it + 1)
                dve.tensor_scalar(z1[:, :], misc[:, :], bias[:, B_1:B_1 + 1], None,
                                  ALU.add).then_inc(z1_ready, 1)
                dve.tensor_scalar(e1[:, :], e1[:, :], 1.0, None, ALU.add).then_inc(silu_step, 1)

            def silu_reciprocal(it, n):
                a = e1[:, n * P:(n + 1) * P]
                if n == 0:
                    dve.wait_ge(silu_step, it * 4 + 1)
                last = dve.reciprocal(a, a)
                if n == BLOCKS - 1:
                    last.then_inc(silu_step, 1)

            def probs_t_out(g, s, first):
                dve.wait_ge(t_done, g * 2 + 2)
                if not (first and s < 2):
                    dve.wait_ge(pv_done, g - 1)
                dve.tensor_copy(probs_t[:, s % 2, 1, PT_FROM:], t_ps[1][:, PT_FROM:]).then_inc(pt_ready[1], 1)

            def group(it, first=False, last=False):
                for s in range(SLOTS):
                    g = it * SLOTS + s
                    row_maxima(g, s, first)
                    if not (first and s == 0):
                        reciprocals(g - 1, (s - 1) % SLOTS)
                    kind, ahead, i = task_a(s)
                    if not (last and ahead):
                        evacuate((kind, it + ahead, i))
                    if not (first and s < 2):
                        probs_t_out(g - 2, (s - 2) % SLOTS, first)
                    b_task = TASK_B.get(s)
                    if present(b_task, first, last):
                        evacuate((b_task[0], it + b_task[1], b_task[2]))
                    if s == MOMENTS_AT and not last:
                        if first:
                            dve.wait_ge(x_rest_in, 16)
                        moments(it + 1, it + 1, stats_done, mv_ready)
                    if s == NORMAL_AT and not last:
                        normal_x(it + 1, it + 1, rstd_ready, xn_ready)
                    if s == SILU_START and not last:
                        silu_start(it + 1)
                    if not last:
                        for n in SILU_AT.get(s, ()):
                            silu_reciprocal(it + 1, n)

            dve.wait_ge(x_in, 16)
            moments(0, 0, stats_done, mv_ready)
            normal_x(0, 0, rstd_ready, xn_ready)
            dve.wait_ge(bias_in, 16)
            dve.tensor_scalar(neg_b1[:, :], bias[:, B_1:B_1 + 1], -1.0, None, ALU.mult)
            dve.wait_ge(w12_in, 32)
            dve.tensor_copy(w_hi[:, W_1:W_G], w_raw[:, W_1:W_G]).then_inc(w12_hi_ready, 1)
            dve.wait_ge(w12_hi_ready, 1)
            low(w_lo[:, W_1:W_G], w_raw[:, W_1:W_G], w_hi[:, W_1:W_G]).then_inc(w12_ready, 1)
            evacuate(("tx", 0, 0))
            silu_start(0)
            for n in range(BLOCKS):
                silu_reciprocal(0, n)
            evacuate(("m2", 0, 0))
            evacuate(("q", 0, 0))
            evacuate(("k", 0, 0))
            evacuate(("q", 0, 1))
            dve.wait_ge(zeros_ready, 2)
            dve.wait_ge(consts_ready, 2)
            group(0, first=True)
            with dve.Fori(1, GROUPS - 1) as it:
                group(it)
            group(GROUPS - 1, last=True)
            n = GROUPS * SLOTS
            reciprocals(n - 1, SLOTS - 1)
            for k in (2, 1):
                probs_t_out(n - k, SLOTS - k, False)
            evacuate(("ty", GROUPS - 1, 0))
            dve.wait_ge(x1_ready, GROUPS)

            def f_xnt_out(c):
                dve.wait_ge(f_xnt_hi, c + 1)
                low(xnt_lo[:, :], bank[0][:, :], xnt_hi[:, :]).then_inc(f_xnt, 1)

            def f_g_out(c, k):
                dve.wait_ge(f_g_hi, c * 3 + k + 1)
                low(o_lo[:, k, :], g_f32[k % 2][:, :], o_hi[:, k, :]).then_inc(f_g, 1)

            def f_residual(c):
                dve.wait_ge(f_ty, c + 1)
                dve.tensor_tensor(x_group(c), bank[6][:, :], x_group(c), ALU.add).then_inc(f_out, 1)

            def f_moments(c):
                moments(c, c, f_stats, f_mv)

            f_moments(0)
            normal_x(0, 0, f_rstd, f_xn)
            dve.wait_ge(f_xn, 1)
            f_moments(1)
            f_xnt_out(0)
            normal_x(1, 1, f_rstd, f_xn)
            for k in range(HCHUNKS - 1):
                f_g_out(0, k)

            def chunk(c, first=False, stats_ahead=True):
                if stats_ahead:
                    f_moments(c + 2)
                f_xnt_out(c + 1)
                if not first:
                    f_residual(c - 1)
                f_g_out(c + 1, 0)
                if stats_ahead:
                    normal_x(c + 2, c + 2, f_rstd, f_xn)
                for k in range(1, HCHUNKS - 1):
                    f_g_out(c + 1, k)

            chunk(0, first=True)
            with dve.Fori(1, GROUPS - 2) as c:
                chunk(c)
            chunk(GROUPS - 2, stats_ahead=False)
            f_residual(GROUPS - 2)
            f_residual(GROUPS - 1)


def kernel(**inputs):
    import numpy as _np
    import concourse.bacc as _bacc
    from concourse import mybir as _mybir
    from concourse.bass_utils import run_bass_kernel_spmd as _run

    a = {k: _np.asarray(t) for k, t in inputs.items()}
    n, dim = BATCH * SEQ, DIM

    def columns(t):
        return t.reshape(-1, P).T

    arrays = {
        "x": a["L0_attn_x"].reshape(n, dim),
        "w1t": a["L0_attn_W1"].T,
        "w2t": a["L0_attn_W2"].T,
        "wgt": a["L0_attn_Wg"].T,
        "wot": a["L0_attn_Wo"].T.reshape(PAIRS, P, dim).transpose(1, 0, 2).reshape(P, PAIRS * dim),
        "fw1": a["L0_ffn_w1"],
        "fw2": a["L0_ffn_w2"].reshape(HCHUNKS, P, dim).transpose(1, 0, 2).reshape(P, HCHUNKS * dim),
        "biases": _np.concatenate([columns(a[k]) for k in (
            "L0_attn_bg", "L0_attn_b1", "L0_attn_b2", "L0_attn_bo", "L0_ffn_b1", "L0_ffn_b2")], axis=1),
    }
    arrays = {k: _np.ascontiguousarray(t) for k, t in arrays.items()}
    nc = _bacc.Bacc("TRN2", target_bir_lowering=False, num_devices=1)
    args = [nc.dram_tensor(f"in_{k}", t.shape, _mybir.dt.from_np(t.dtype), kind="ExternalInput").ap()
            for k, t in arrays.items()]
    out = nc.dram_tensor("out_0", (n, dim), F32, kind="ExternalOutput").ap()
    preln_block(nc, *args, out)
    r = _run(nc, [{f"in_{k}": t for k, t in arrays.items()}], core_ids=[0])
    return r.results[0]["out_0"].reshape(BATCH, SEQ, DIM)
```

```python
from contextlib import ExitStack

import concourse.bass as bass
from concourse import mybir

F32 = mybir.dt.float32
F32R = mybir.dt.float32r
ACT = mybir.ActivationFunctionType
ALU = mybir.AluOpType

P = 128
BATCH, SEQ, DIM = 32, 256, 128
HEADS, HEAD_DIM, WINDOW = 16, 64, 64
HIDDEN = 512
PAIRS = HEADS // 2
GROUP = 2 * SEQ
BLOCKS = GROUP // P
GROUPS = BATCH * SEQ // GROUP
SLOTS = 2 * PAIRS
HCHUNKS = HIDDEN // P
SCALE = HEAD_DIM ** -0.5
EPS = 1e-5
MASKED = -3.0e38

KEYS = [min(SEQ, P * (i + 1) + WINDOW) for i in range(2)]
M_OFF = [0, KEYS[0]]
PT_FROM = P - WINDOW

B_QKV, B_1, B_2, B_O, B_F1, B_F2 = 0, 24, 25, 26, 27, 31
N_BIAS = 32
W_1, W_2, W_G, W_V, W_O, W_F1, W_F2 = 0, 128, 256, 2304, 3328, 4352, 4864
N_W = 5376


def preln_block(nc, x, w1t, w2t, wgt, wot, fw1, fw2, biases, out):
    ctx = ExitStack()
    with ctx:
        def sb(name, shape, dt=F32):
            return ctx.enter_context(nc.sbuf_tensor(name, shape, dt))

        def sem(name):
            return ctx.enter_context(nc.semaphore(name))

        x_all = sb("x_all", [P, GROUPS * BLOCKS * DIM])
        bias = sb("bias", [P, N_BIAS])
        neg_b1 = sb("neg_b1", [P, 1])
        w_hi = sb("w_hi", [P, N_W], F32R)
        w_lo = sb("w_lo", [P, N_W], F32R)
        work = sb("work", [P, 12 * 512])
        w_raw = work[:, 0:W_O]
        late_raw = sb("late_raw", [P, N_W - W_O])
        probs = work[:, 0:8 * 512].rearrange("p (r h c) -> p r h c", r=4, h=2)
        probs_t = work[:, 8 * 512:12 * 512].rearrange("p (r h c) -> p r h c", r=2, h=2)
        ident = sb("ident", [P, P])
        mask = sb("mask", [P, sum(KEYS)])
        stats = sb("stats", [P, BLOCKS, 6])
        mean_var = sb("mean_var", [P, BLOCKS, 2])
        var_eps = sb("var_eps", [P, BLOCKS])
        rstd = sb("rstd", [P, BLOCKS])
        minus_half = sb("minus_half", [P, BLOCKS])
        xn = sb("xn", [P, BLOCKS, DIM])
        xnt_hi = sb("xnt_hi", [P, GROUP], F32R)
        xnt_lo = sb("xnt_lo", [P, GROUP], F32R)
        z1 = sb("z1", [P, GROUP])
        e1 = sb("e1", [P, GROUP])
        s_hi = sb("s_hi", [P, GROUP], F32R)
        s_lo = sb("s_lo", [P, GROUP], F32R)
        h_hi = sb("h_hi", [P, GROUP], F32R)
        h_lo = sb("h_lo", [P, GROUP], F32R)
        q_hi = sb("q_hi", [P, 2, GROUP], F32R)
        q_lo = sb("q_lo", [P, 2, GROUP], F32R)
        k_hi = sb("k_hi", [P, 2, 2, GROUP], F32R)
        k_lo = sb("k_lo", [P, 2, 2, GROUP], F32R)
        v = sb("v", [P, BLOCKS, HEADS * HEAD_DIM])
        o_f32 = sb("o_f32", [P, 2, SEQ])
        o_hi = sb("o_hi", [P, HCHUNKS, GROUP], F32R)
        o_lo = sb("o_lo", [P, HCHUNKS, GROUP], F32R)
        y = sb("y", [P, GROUP])
        row_max = sb("row_max", [P, 4, 4])
        neg_max = sb("neg_max", [P, 4, 4])
        row_sum = sb("row_sum", [P, 4, 4])
        inv_sum = sb("inv_sum", [P, 4, 4])
        table_probe = sb("table_probe", [P, BLOCKS])
        g_f32 = [z1[:, :], e1[:, :], v[:, 0, 0:GROUP], v[:, 1, 0:GROUP]]
        f_xnt_parts = [(xnt_hi[:, :], xnt_lo[:, :]), (s_hi[:, :], s_lo[:, :])]

        bank = [ctx.enter_context(nc.psum_tensor(f"bank{i}", [P, 512], F32)) for i in range(8)]
        s_ps = bank[0:2]
        t_ps = bank[2:4]
        pv_ps = bank[4]
        o_ps = bank[5]
        qk_ps = bank[6]
        misc = bank[7]
        f_hid_ps, f_down_ps, f_xt_ps, f_yt_ps = bank[0:4], bank[4:6], bank[6], bank[7]

        x_in, x_1_in, x_rest_in, w12_in, wg_in, wof_in, bias_in = map(
            sem, ("x_in", "x_1_in", "x_rest_in", "w12_in", "wg_in", "wof_in", "bias_in"))
        consts_ready = sem("consts_ready")
        zeros_ready = sem("zeros_ready")
        w12_hi_ready, w12_ready = sem("w12_hi_ready"), sem("w12_ready")
        wg_hi_ready, wg_ready = sem("wg_hi_ready"), sem("wg_ready")
        wof_hi_ready, wof_ready = sem("wof_hi_ready"), sem("wof_ready")
        stats_done, mv_ready = sem("stats_done"), sem("mv_ready")
        rstd_step, rstd_ready, xn_ready = sem("rstd_step"), sem("rstd_ready"), sem("xn_ready")
        tx_done, xnt_hi_ready, xnt_ready = sem("tx_done"), sem("xnt_hi_ready"), sem("xnt_ready")
        m1_done, e1_ready, z1_ready = sem("m1_done"), sem("e1_ready"), sem("z1_ready")
        silu_step, s_ready = sem("silu_step"), sem("s_ready")
        silu0_step, s0_hi_ready = sem("silu0_step"), sem("s0_hi_ready")
        m2_done, h_hi_ready, h_ready = sem("m2_done"), sem("h_hi_ready"), sem("h_ready")
        q_done, q_hi_ready, q_ready = sem("q_done"), sem("q_hi_ready"), sem("q_ready")
        k_done, k_hi_ready, k_ready = sem("k_done"), sem("k_hi_ready"), sem("k_ready")
        v_done, v_ready = sem("v_done"), sem("v_ready")
        s_done = sem("s_done")
        max_done, neg_ready = sem("max_done"), sem("neg_ready")
        exp_done, inv_ready, norm_done = sem("exp_done"), sem("inv_ready"), sem("norm_done")
        t_done = sem("t_done")
        pt_ready = [sem("pt0_ready"), sem("pt1_ready")]
        pv_done, o_hi_ready, o_ready = sem("pv_done"), sem("o_hi_ready"), sem("o_ready")
        o_f32_ready = sem("o_f32_ready")
        om_done, y_ready, ty_done, x1_ready = sem("om_done"), sem("y_ready"), sem("ty_done"), sem("x1_ready")
        f_stats, f_mv, f_rstd_step = sem("f_stats"), sem("f_mv"), sem("f_rstd_step")
        f_rstd, f_xn = sem("f_rstd"), sem("f_xn")
        f_tx, f_xnt_hi, f_xnt = sem("f_tx"), sem("f_xnt_hi"), sem("f_xnt")
        f_m1, f_gelu_done, f_g_hi, f_g = sem("f_m1"), sem("f_gelu_done"), sem("f_g_hi"), sem("f_g")
        f_g_pool_hi, f_g_pool = sem("f_g_pool_hi"), sem("f_g_pool")
        f_m2, f_y, f_ty, f_out = sem("f_m2"), sem("f_y"), sem("f_ty"), sem("f_out")
        stored = sem("stored")
        dve_passed, pool_passed = sem("dve_passed"), sem("pool_passed")

        def split_product(eng, out_ap, w, a, first=True, last=True):
            eng.matmul(out_ap, w[0], a[0], start=first, stop=False)
            eng.matmul(out_ap, w[0], a[1], start=False, stop=False)
            return eng.matmul(out_ap, w[1], a[0], start=False, stop=last)

        def w_parts(at, n=P):
            return w_hi[:, at:at + n], w_lo[:, at:at + n]

        def x_group(it):
            return x_all[:, bass.ds(it * (BLOCKS * DIM), BLOCKS * DIM)]

        def x_block(it, b):
            return x_all[:, bass.ds(it * (BLOCKS * DIM) + b * DIM, DIM)]

        FIRST_K_PS, FIRST_Q1_PS, FIRST_V1_PS = o_ps, t_ps[0], pv_ps
        WARM = (2, 1, 6, 1)

        x_v = x.rearrange("(n p) d -> p n d", p=P)
        out_v = out.rearrange("(n p) d -> p n d", p=P)
        block = ctx.enter_context(nc.Block())

        def task_a(s):
            kind, pair = ("q", (s + 3) // 2) if s % 2 else ("k", (s + 2) // 2)
            return kind, pair // PAIRS, pair % PAIRS

        TASK_B = {0: ("v", 0, 2), 1: ("v", 0, 3), 2: ("v", 0, 4), 3: ("tx", 1, 0), 4: ("m1", 1, 0),
                  6: ("v", 0, 5), 7: ("v", 0, 6), 8: ("v", 0, 7), 9: ("ty", -1, 0),
                  12: ("m2", 1, 0), 14: ("v", 1, 0), 15: ("v", 1, 1)}

        def out_pair(s):
            if s % 2 == 0:
                return None
            pair = (s - 7) // 2
            return (0, pair) if pair >= 0 else (-1, pair + PAIRS)

        MOMENTS_AT, DEVIATIONS_AT, NORMAL_AT = 0, 1, 2
        F_MOMENTS_AT, F_DEVIATIONS_AT, F_NORMAL_AT = 5, 6, 7
        SILU_AT = {6: (0,), 7: (1, 2), 8: (3,)}
        SILU_START, SILU_PRODUCT, SILU_PARTS = 5, 9, 10

        EARLY_B = (12,)

        def present(task, first, last):
            return (task is not None and not (first and task[1] < 0)
                    and not (last and task[1] > 0 and task[0] != "tx"))

        def f_steps(eng, step):
            for c in range(2):
                step(c, c % 2)
            with eng.Fori(1, (GROUPS - 4) // 2) as m:
                for odd in range(2):
                    step(m * 2 + odd, odd)
            for c in range(GROUPS - 4, GROUPS):
                step(c, c % 2, left=min(3, GROUPS - 1 - c))

        @block.sync
        def _(sp):
            def load_x(first, end, done):
                sp.dma_start(x_all[:, first * BLOCKS * DIM:end * BLOCKS * DIM].rearrange("p (n d) -> p n d", d=DIM),
                             x_v[:, first * BLOCKS:end * BLOCKS, :]).then_inc(done, 16)

            load_x(0, 1, x_in)
            sp.dma_start(w_raw[:, W_1:W_1 + P], w1t).then_inc(w12_in, 16)
            sp.dma_start(w_raw[:, W_2:W_2 + P], w2t).then_inc(w12_in, 16)
            sp.dma_start(bias[:, :], biases).then_inc(bias_in, 16)
            sp.dma_start(w_raw[:, W_G:W_O], wgt).then_inc(wg_in, 16)
            load_x(1, 2, x_1_in)
            sp.dma_start(late_raw[:, 0:W_F1 - W_O], wot).then_inc(wof_in, 16)
            sp.dma_start(late_raw[:, W_F1 - W_O:W_F2 - W_O], fw1).then_inc(wof_in, 16)
            sp.dma_start(late_raw[:, W_F2 - W_O:N_W - W_O], fw2).then_inc(wof_in, 16)
            load_x(2, GROUPS, x_rest_in)

            def store(c):
                sp.wait_ge(f_out, c + 1)
                sp.dma_start(out_v[:, bass.ds(c * BLOCKS, BLOCKS), :],
                             x_group(c).rearrange("p (n d) -> p n d", d=DIM)).then_inc(stored, 16)

            with sp.Fori(0, GROUPS) as c:
                store(c)
            sp.wait_ge(stored, 16 * GROUPS)

        @block.gpsimd
        def _(pool):
            pool.memset(ident[:, :], 0.0)
            pool.memset(minus_half[:, :], -0.5)
            pool.memset(mask[:, :], 0.0).then_inc(consts_ready, 1)
            pool.wait_ge(consts_ready, 1)
            pool.affine_select(out=ident[:, :], in_=ident[:, :], compare_op=ALU.not_equal, fill=1.0,
                               base=0, pattern=[[-1, P]], channel_multiplier=1)
            for i in range(2):
                m = mask[:, M_OFF[i]:M_OFF[i] + KEYS[i]]
                last = pool.affine_select(out=m, in_=m, compare_op=ALU.is_ge, fill=MASKED,
                                          base=P * i + WINDOW - 1, pattern=[[-1, KEYS[i]]],
                                          channel_multiplier=1)
            last.then_inc(consts_ready, 1)

            def inverse_deviations(n, moments, step, ready):
                pool.wait_ge(moments, n + 1)
                pool.sem_inc(pool_passed, 1)
                pool.tensor_scalar(var_eps[:, :], mean_var[:, :, 1], EPS, 1.0, ALU.add,
                                   ALU.mult).then_inc(step, 1)
                pool.wait_ge(step, n + 1)
                pool.tensor_tensor(rstd[:, :], var_eps[:, :], minus_half[:, :], ALU.pow).then_inc(ready, 1)

            def normalise(g, s):
                pool.wait_ge(inv_ready, g + 1)
                pool.sem_inc(pool_passed, 1)
                for hd in range(2):
                    for i in range(2):
                        a = probs[:, s % 4, hd, SEQ * i:SEQ * i + KEYS[i]]
                        last = pool.tensor_scalar(a, a, inv_sum[:, s % 4, 2 * hd + i:2 * hd + i + 1], 1.0,
                                                  ALU.mult, ALU.mult)
                last.then_inc(norm_done, 1)

            def values_parts(g, s):
                p, cols = s // 2 % 2, slice(s % 2 * SEQ, s % 2 * SEQ + SEQ)
                pool.wait_ge(o_f32_ready, g + 1)
                pool.sem_inc(pool_passed, 1)
                pool.tensor_scalar(o_hi[:, p, cols], o_f32[:, s % 2, :], 1.0, 1.0, ALU.mult,
                                   ALU.mult).then_inc(o_hi_ready, 1)
                pool.wait_ge(o_hi_ready, g + 1)
                pool.tensor_tensor(o_lo[:, p, cols], o_f32[:, s % 2, :], o_hi[:, p, cols].bitcast(F32),
                                   ALU.subtract).then_inc(o_ready, 1)

            def silu_product(it):
                pool.wait_ge(silu_step, it * 4 - 1)
                pool.tensor_tensor(z1[:, :], z1[:, :], e1[:, :], ALU.mult).then_inc(silu_step, 1)

            def silu_parts(it):
                pool.wait_ge(silu_step, it * 4)
                pool.sem_inc(pool_passed, 1)
                pool.tensor_scalar(s_hi[:, :], z1[:, :], 1.0, 1.0, ALU.mult, ALU.mult).then_inc(silu_step, 1)
                pool.wait_ge(silu_step, it * 4 + 1)
                pool.tensor_tensor(s_lo[:, :], z1[:, :], s_hi[:, :].bitcast(F32),
                                   ALU.subtract).then_inc(s_ready, 1)

            def group(it, first=False, last=False):
                for s in range(SLOTS):
                    late = s == SILU_PARTS + 1
                    if not late and not (first and s < 4):
                        values_parts(it * SLOTS + s - 4, (s - 4) % SLOTS)
                    if not (first and s == 0):
                        normalise(it * SLOTS + s - 1, (s - 1) % SLOTS)
                    if late:
                        values_parts(it * SLOTS + s - 4, (s - 4) % SLOTS)
                    if s == SILU_PRODUCT and not last:
                        silu_product(it + 1)
                    if s == SILU_PARTS and not last:
                        silu_parts(it + 1)
                    if s == DEVIATIONS_AT:
                        inverse_deviations(it + 1, mv_ready, rstd_step, rstd_ready)
                    if s == F_DEVIATIONS_AT and last:
                        inverse_deviations(0, f_mv, f_rstd_step, f_rstd)

            inverse_deviations(0, mv_ready, rstd_step, rstd_ready)
            pool.memset(k_hi[:, :, :, :].bitcast(F32), 0.0)
            pool.memset(k_lo[:, :, :, :].bitcast(F32), 0.0).then_inc(zeros_ready, 1)
            for n, (a, b) in enumerate(((W_G, W_V), (W_V, W_O))):
                pool.wait_ge(wg_hi_ready, n + 1)
                pool.tensor_tensor(w_lo[:, a:b], w_raw[:, a:b], w_hi[:, a:b].bitcast(F32),
                                   ALU.subtract).then_inc(wg_ready, 1)
            pool.wait_ge(wg_ready, 2)
            pool.wait_ge(w12_ready, 1)
            pool.memset(probs[:, :, :, KEYS[0]:SEQ], 0.0).then_inc(zeros_ready, 1)
            pool.wait_ge(wof_in, 48)
            pool.tensor_scalar(w_hi[:, W_O:N_W], late_raw[:, :], 1.0, 1.0, ALU.mult,
                               ALU.mult).then_inc(wof_hi_ready, 1)
            pool.wait_ge(wof_hi_ready, 1)
            pool.tensor_tensor(w_lo[:, W_O:N_W], late_raw[:, :], w_hi[:, W_O:N_W].bitcast(F32),
                               ALU.subtract).then_inc(wof_ready, 1)
            group(0, first=True)
            with pool.Fori(1, GROUPS - 1) as it:
                group(it)
            group(GROUPS - 1, last=True)
            n = GROUPS * SLOTS
            values_parts(n - 4, SLOTS - 4)
            normalise(n - 1, SLOTS - 1)
            for k in (3, 2, 1):
                values_parts(n - k, SLOTS - k)

            def f_g_parts(c):
                k = HCHUNKS - 1
                pool.wait_ge(f_gelu_done, (c + 1) * HCHUNKS)
                pool.sem_inc(pool_passed, 1)
                pool.tensor_scalar(o_hi[:, k, :], g_f32[k], 1.0, 1.0, ALU.mult,
                                   ALU.mult).then_inc(f_g_pool_hi, 1)
                pool.wait_ge(f_g_pool_hi, c + 1)
                pool.tensor_tensor(o_lo[:, k, :], g_f32[k], o_hi[:, k, :].bitcast(F32),
                                   ALU.subtract).then_inc(f_g_pool, 1)

            def step(c, odd, left=3):
                if left >= 3:
                    inverse_deviations(c + 2, f_mv, f_rstd_step, f_rstd)
                if left:
                    f_g_parts(c + 1)

            inverse_deviations(1, f_mv, f_rstd_step, f_rstd)
            f_g_parts(0)
            f_steps(pool, step)

        @block.tensor
        def _(pe):
            def free(task):
                kind, it, i = task
                if kind in "qkv":
                    pe.wait_ge({"q": q_ready, "k": k_ready, "v": v_ready}[kind], it * 8 + i + 1)
                else:
                    pe.wait_ge({"tx": xnt_ready, "m1": z1_ready, "m2": h_ready,
                                "ty": x1_ready}[kind], it + 1)

            def do(task, ps=None):
                kind, it, i = task
                ps = (qk_ps if kind in "qk" else misc) if ps is None else ps
                if kind == "tx":
                    pe.wait_ge(xn_ready, it + 1)
                    for b in range(BLOCKS):
                        last = pe.transpose(misc[:, b * P:(b + 1) * P], xn[:, b, :], ident[:, :])
                    last.then_inc(tx_done, 1)
                elif kind == "m1":
                    pe.wait_ge(xnt_ready, it + 1)
                    split_product(pe, ps[:, :], w_parts(W_1), (xnt_hi[:, :], xnt_lo[:, :])).then_inc(m1_done, 1)
                elif kind == "m2":
                    pe.wait_ge(s_ready, it + 1)
                    split_product(pe, ps[:, :], w_parts(W_2), (s_hi[:, :], s_lo[:, :])).then_inc(m2_done, 1)
                elif kind in "qk":
                    pe.wait_ge(h_ready, it + 1)
                    at = W_G + (kind == "k") * HEADS * HEAD_DIM + i * P
                    split_product(pe, ps[:, :], w_parts(at), (h_hi[:, :], h_lo[:, :])).then_inc(
                        q_done if kind == "q" else k_done, 1)
                elif kind == "v":
                    pe.wait_ge(h_ready, it + 1)
                    b, at = i % 4, W_V + i // 4 * 512
                    cols = slice(b * P, (b + 1) * P)
                    split_product(pe, ps[:, :], (h_hi[:, cols], h_lo[:, cols]),
                                  w_parts(at, 512)).then_inc(v_done, 1)
                elif kind == "ty":
                    pe.wait_ge(y_ready, it + 1)
                    for b in range(BLOCKS):
                        last = pe.transpose(misc[:, b * P:(b + 1) * P], y[:, b * P:(b + 1) * P], ident[:, :])
                    last.then_inc(ty_done, 1)

            def out_projection(it, p, first):
                pe.wait_ge(o_ready, it * SLOTS + 2 * p + 2)
                if p == 0 and not first:
                    pe.wait_ge(y_ready, it)
                last = split_product(pe, o_ps[:, :], w_parts(W_O + p * P),
                                     (o_hi[:, p % 2, :], o_lo[:, p % 2, :]), first=p == 0, last=p == PAIRS - 1)
                if p == PAIRS - 1:
                    last.then_inc(om_done, 1)

            def scores(it, s, first):
                g, p, b = it * SLOTS + s, s // 2, s % 2
                pe.wait_ge(q_ready, it * 8 + p + 1)
                pe.wait_ge(k_ready, it * 8 + p + 1)
                for i in range(2):
                    if not (first and s == 0):
                        pe.wait_ge(max_done, g * 2 - 1 + i)
                    dst = s_ps[i][:, 0:2 * KEYS[i]].rearrange("p (h c) -> p h c", h=2)
                    rows = slice(b * SEQ + i * P, b * SEQ + (i + 1) * P)
                    cols = slice(b * SEQ, b * SEQ + KEYS[i])
                    split_product(pe, dst, (q_hi[:, p % 2, rows], q_lo[:, p % 2, rows]),
                                  (k_hi[:, p % 2, :, cols], k_lo[:, p % 2, :, cols])).then_inc(s_done, 1)

            def transposes(it, s, first):
                g = it * SLOTS + s
                pe.wait_ge(norm_done, g + 1)
                for hd in range(2):
                    if not (first and s == 0):
                        pe.wait_ge(pt_ready[hd], g)
                    for n, j in enumerate((1, 0)):
                        for i in (1, 0):
                            q = PT_FROM * (i < j)
                            last = pe.transpose(t_ps[hd][:, SEQ * n + P * i + q:SEQ * n + P * (i + 1)],
                                                probs[q:, s % 4, hd, SEQ * i + P * j:SEQ * i + P * (j + 1)],
                                                ident[q:, q:])
                    last.then_inc(t_done, 1)

            def values(it, s, first):
                g, p, b = it * SLOTS + s, s // 2, s % 2
                for hd in range(2):
                    pe.wait_ge(pt_ready[hd], g + 1)
                pe.wait_ge(v_ready, it * 8 + p // 4 * 4 + 2 * b + 2)
                if not (first and s == 0):
                    pe.wait_ge(o_f32_ready, g)
                for j in range(2):
                    for hd in (j, 1 - j):
                        head = (2 * p + hd) * HEAD_DIM
                        dst = pv_ps[hd * HEAD_DIM:(hd + 1) * HEAD_DIM, PT_FROM * j:SEQ]
                        src = probs_t[:, s % 2, hd, (SEQ, PT_FROM)[j]:(2 * SEQ, SEQ)[j]]
                        last = pe.matmul(dst, v[:, 2 * b + j, head:head + HEAD_DIM], src,
                                         start=j == 0, stop=j == 1)
                last.then_inc(pv_done, 1)

            def group(it, first=False, last=False):
                prev_a, prev = ("q", it, 1), ("v", it, 1)
                for s in range(SLOTS):
                    scores(it, s, first)
                    kind, ahead, i = task_a(s)
                    if not (last and ahead):
                        free(prev_a)
                        prev_a = (kind, it + ahead, i)
                        do(prev_a)
                    before, same = (it, True) if s >= 2 else (it - 1, False)
                    if same or not first:
                        transposes(before, (s - 2) % SLOTS, first and same)
                    if s == 7 and first:
                        pe.wait_ge(wof_ready, 1)
                    if out_pair(s) and not (first and out_pair(s)[0]):
                        out_projection(it + out_pair(s)[0], out_pair(s)[1], first)
                    b_task = TASK_B.get(s)
                    for now in (True, False):
                        if present(b_task, first, last) and now == (s in EARLY_B):
                            free(prev)
                            prev = (b_task[0], it + b_task[1], b_task[2])
                            do(prev)
                        before, same = (it, True) if s >= 3 else (it - 1, False)
                        if now and (same or not first):
                            values(before, (s - 3) % SLOTS, first and same)
                return prev

            def keep_warm(n):
                for _ in range(n):
                    pe.matmul(bank[0][:, :], ident[:, :], x_group(0), start=True, stop=True)

            pe.wait_ge(consts_ready, 2)
            pe.wait_ge(x_in, 16)
            keep_warm(WARM[0])
            do(("tx", 0, 0))
            keep_warm(WARM[1])
            pe.wait_ge(w12_ready, 1)
            do(("m1", 0, 0))
            keep_warm(WARM[2])
            do(("m2", 0, 0))
            keep_warm(WARM[3])
            pe.wait_ge(wg_ready, 1)
            do(("k", 0, 0), FIRST_K_PS)
            do(("q", 0, 0))
            pe.wait_ge(wg_ready, 2)
            do(("v", 0, 0))
            do(("q", 0, 1), FIRST_Q1_PS)
            do(("v", 0, 1), FIRST_V1_PS)
            pe.wait_ge(zeros_ready, 1)
            group(0, first=True)
            with pe.Fori(1, GROUPS - 1) as it:
                group(it)
            end = GROUPS - 1
            prev = group(end, last=True)
            transposes(end, SLOTS - 2, False)

            def f_transpose_x(c):
                pe.wait_ge(f_xn, c)
                for b in range(BLOCKS):
                    last = pe.transpose(f_xt_ps[:, b * P:(b + 1) * P], xn[:, b, :], ident[:, :])
                last.then_inc(f_tx, 1)

            def f_hidden(c, odd, k):
                if k == 0:
                    pe.wait_ge(f_xnt, c)
                split_product(pe, f_hid_ps[k][:, :], w_parts(W_F1 + k * P), f_xnt_parts[odd]).then_inc(f_m1, 1)

            def f_down(c, odd, k):
                if k == HCHUNKS - 1:
                    pe.wait_ge(f_g_pool, c + 1)
                else:
                    pe.wait_ge(f_g, c * 3 + k + 1)
                last = split_product(pe, f_down_ps[odd][:, :], w_parts(W_F2 + k * P),
                                     (o_hi[:, k, :], o_lo[:, k, :]), first=k == 0, last=k == HCHUNKS - 1)
                if k == HCHUNKS - 1:
                    last.then_inc(f_m2, 1)

            def f_transpose_y(c):
                pe.wait_ge(f_y, c + 1)
                if not (isinstance(c, int) and c < 1):
                    pe.wait_ge(f_out, c)
                for b in range(BLOCKS):
                    last = pe.transpose(f_yt_ps[:, b * P:(b + 1) * P], y[:, b * P:(b + 1) * P], ident[:, :])
                last.then_inc(f_ty, 1)

            def step(c, odd, left=3):
                for k in range(HCHUNKS):
                    if k == 2 and not (isinstance(c, int) and c < 1):
                        f_transpose_y(c - 1)
                    if k == 3 and left >= 2:
                        f_transpose_x(c + 2)
                    f_down(c, odd, k)
                    if left and not (isinstance(c, int) and c < 1 and k < 2):
                        f_hidden(c + 1, 1 - odd, k)

            def first_hidden(k):
                split_product(pe, f_hid_ps[k][:, :], w_parts(W_F1 + k * P), f_xnt_parts[0]).then_inc(f_m1, 1)

            pe.wait_ge(xnt_ready, GROUPS + 1)
            pe.wait_ge(max_done, (end + 1) * SLOTS * 2)
            first_hidden(0)
            values(end, SLOTS - 3, False)
            f_transpose_x(1)
            first_hidden(1)
            transposes(end, SLOTS - 1, False)
            out_projection(end, PAIRS - 3, False)
            values(end, SLOTS - 2, False)
            pe.wait_ge(pt_ready[0], (end + 1) * SLOTS)
            first_hidden(2)
            pe.wait_ge(pt_ready[1], (end + 1) * SLOTS)
            first_hidden(3)
            values(end, SLOTS - 1, False)
            out_projection(end, PAIRS - 2, False)
            for k in range(2):
                pe.wait_ge(f_gelu_done, k + 1)
                f_hidden(1, 1, k)
            out_projection(end, PAIRS - 1, False)
            free(prev)
            do(("ty", end, 0))
            pe.wait_ge(o_f32_ready, (end + 1) * SLOTS)
            f_steps(pe, step)
            f_transpose_y(GROUPS - 1)

        @block.scalar
        def _(act):
            def identity(dst, src, col, rows=slice(0, P)):
                return act.activation(dst, src, ACT.Identity, bias=bias[rows, col:col + 1])

            def exponentials(g, s, first):
                act.wait_ge(neg_ready, g + 1)
                for hd in range(2):
                    for i in range(2):
                        n = 2 * hd + i
                        a = probs[:, s % 4, hd, SEQ * i:SEQ * i + KEYS[i]]
                        last = act.activation(a, a, ACT.Exp, bias=neg_max[:, s % 4, n:n + 1], scale=SCALE,
                                              accum_out=row_sum[:, s % 4, n:n + 1])
                last.then_inc(exp_done, 1)

            def evacuate(task, ps=None):
                kind, it, i = task
                ps = (qk_ps if kind in "qk" else misc) if ps is None else ps
                if kind == "q":
                    act.wait_ge(q_done, it * 8 + i + 1)
                    identity(q_hi[:, i % 2, :], ps[:, :], B_QKV + i).then_inc(q_hi_ready, 1)
                elif kind == "k":
                    act.wait_ge(k_done, it * 8 + i + 1)
                    for hd in range(2):
                        rows = slice(hd * HEAD_DIM, (hd + 1) * HEAD_DIM)
                        identity(k_hi[rows, i % 2, hd, :], ps[rows, :], B_QKV + PAIRS + i, rows).then_inc(
                            k_hi_ready, 1)
                elif kind == "v":
                    act.wait_ge(v_done, it * 8 + i + 1)
                    act.copy(v[:, i % 4, i // 4 * 512:i // 4 * 512 + 512], ps[:, :]).then_inc(v_ready, 1)
                elif kind == "tx":
                    act.wait_ge(tx_done, it + 1)
                    act.copy(xnt_hi[:, :], ps[:, :]).then_inc(xnt_hi_ready, 1)
                elif kind == "m1":
                    act.wait_ge(m1_done, it + 1)
                    act.activation(e1[:, :], ps[:, :], ACT.Exp, bias=neg_b1[:, 0:1], scale=-1.0).then_inc(
                        e1_ready, 1)
                elif kind == "m2":
                    act.wait_ge(m2_done, it + 1)
                    identity(h_hi[:, :], ps[:, :], B_2).then_inc(h_hi_ready, 1)

            def probs_t_out(g, s, first):
                act.wait_ge(t_done, g * 2 + 1)
                if not (first and s < 2):
                    act.wait_ge(pv_done, g - 1)
                act.copy(probs_t[:, s % 2, 0, PT_FROM:], t_ps[0][:, PT_FROM:]).then_inc(pt_ready[0], 1)

            def values_out(g, s, first):
                act.wait_ge(pv_done, g + 1)
                if not (first and s < 2):
                    act.wait_ge(o_ready, g - 1)
                identity(o_f32[:, s % 2, :], pv_ps[:, 0:SEQ], B_QKV + 2 * PAIRS + s // 2).then_inc(
                    o_f32_ready, 1)

            def projection_out(it):
                act.wait_ge(om_done, it + 1)
                identity(y[:, :], o_ps[:, :], B_O).then_inc(y_ready, 1)

            def group(it, first=False, last=False):
                for s in range(SLOTS):
                    g = it * SLOTS + s
                    if not (first and s == 0):
                        exponentials(g - 1, (s - 1) % SLOTS, first)
                    kind, ahead, i = task_a(s)
                    if not (last and ahead):
                        evacuate((kind, it + ahead, i))
                    if not (first and s < 2):
                        probs_t_out(g - 2, (s - 2) % SLOTS, first)
                    if s == 5 and not first:
                        projection_out(it - 1)
                    b_task = TASK_B.get(s)
                    for now in (True, False):
                        if present(b_task, first, last) and now == (s in EARLY_B):
                            evacuate((b_task[0], it + b_task[1], b_task[2]))
                        if now and not (first and s < 3):
                            values_out(g - 3, (s - 3) % SLOTS, first)

            act.wait_ge(consts_ready, 2)
            act.activation(table_probe[:, :], minus_half[:, :], ACT.Exp)
            act.wait_ge(bias_in, 16)
            evacuate(("tx", 0, 0))
            act.wait_ge(wg_in, 16)
            act.copy(w_hi[:, W_G:W_V], w_raw[:, W_G:W_V]).then_inc(wg_hi_ready, 1)
            act.wait_ge(w12_ready, 1)
            evacuate(("m1", 0, 0))
            act.copy(w_hi[:, W_V:W_O], w_raw[:, W_V:W_O]).then_inc(wg_hi_ready, 1)
            for half in range(2):
                cols = slice(half * SEQ, half * SEQ + SEQ)
                act.wait_ge(silu0_step, 2 * half + 2)
                act.copy(s_hi[:, cols], z1[:, cols]).then_inc(s0_hi_ready, 1)
            evacuate(("m2", 0, 0))
            act.wait_ge(zeros_ready, 1)
            evacuate(("k", 0, 0), FIRST_K_PS)
            evacuate(("q", 0, 0))
            evacuate(("v", 0, 0))
            evacuate(("q", 0, 1), FIRST_Q1_PS)
            evacuate(("v", 0, 1), FIRST_V1_PS)
            group(0, first=True)
            with act.Fori(1, GROUPS - 1) as it:
                group(it)
            group(GROUPS - 1, last=True)
            n = GROUPS * SLOTS
            exponentials(n - 1, SLOTS - 1, False)

            def f_xnt_out(c, odd):
                act.wait_ge(f_tx, c)
                act.copy(f_xnt_parts[odd][0], f_xt_ps[:, :]).then_inc(f_xnt_hi, 1)

            def f_gelu(c, k):
                act.wait_ge(f_m1, c * HCHUNKS + k + 1)
                act.activation(g_f32[k], f_hid_ps[k][:, :], ACT.Gelu,
                               bias=bias[:, B_F1 + k:B_F1 + k + 1]).then_inc(f_gelu_done, 1)

            def f_g_high(c, k):
                act.wait_ge(f_gelu_done, c * HCHUNKS + k + 1)
                act.copy(o_hi[:, k, :], g_f32[k]).then_inc(f_g_hi, 1)

            def f_y_out(c, odd):
                act.wait_ge(f_m2, c + 1)
                identity(y[:, :], f_down_ps[odd][:, :], B_F2).then_inc(f_y, 1)

            def step(c, odd, left=3):
                if isinstance(c, int) and c < 1:
                    for k in range(2):
                        act.wait_ge(f_g, k + 1)
                        f_gelu(1, k)
                    act.wait_ge(f_g, 3)
                    f_gelu(1, 2)
                    f_g_high(1, 0)
                    f_g_high(1, 1)
                elif left:
                    f_y_out(c - 1, 1 - odd)
                    f_gelu(c + 1, 0)
                    f_g_high(c + 1, 0)
                    f_gelu(c + 1, 1)
                    f_g_high(c + 1, 1)
                    f_gelu(c + 1, 2)
                else:
                    f_y_out(c - 1, 1 - odd)
                if left:
                    if left >= 2:
                        f_xnt_out(c + 2, odd)
                    f_g_high(c + 1, 2)
                    f_gelu(c + 1, 3)

            probs_t_out(n - 2, SLOTS - 2, False)
            values_out(n - 3, SLOTS - 3, False)
            f_xnt_out(1, 1)
            probs_t_out(n - 1, SLOTS - 1, False)
            values_out(n - 2, SLOTS - 2, False)
            f_gelu(0, 0)
            values_out(n - 1, SLOTS - 1, False)
            f_gelu(0, 1)
            f_gelu(0, 2)
            f_gelu(0, 3)
            projection_out(GROUPS - 1)
            for k in range(HCHUNKS - 1):
                f_g_high(0, k)
            f_steps(act, step)
            f_y_out(GROUPS - 1, 1)

        @block.vector
        def _(dve):
            def low(dst, src, hi, col=None, rows=slice(0, P)):
                if col is None:
                    return dve.tensor_tensor(dst, src, hi.bitcast(F32), ALU.subtract)
                return dve.scalar_tensor_tensor(out=dst, in0=src, scalar=bias[rows, col:col + 1],
                                                in1=hi.bitcast(F32), op0=ALU.add, op1=ALU.subtract)

            def moments(it, n, step, ready):
                for b in range(BLOCKS):
                    last = dve.bn_stats(stats[:, b, :], x_block(it, b))
                last.then_inc(step, 1)
                dve.wait_ge(step, n + 1)
                dve.sem_inc(dve_passed, 1)
                for b in range(BLOCKS):
                    last = dve.bn_aggr(mean_var[:, b, :], stats[:, b, :])
                last.then_inc(ready, 1)

            def normal_x(it, n, rstd_done, ready):
                dve.wait_ge(rstd_done, n + 1)
                for b in range(BLOCKS):
                    last = dve.tensor_scalar(xn[:, b, :], x_block(it, b), mean_var[:, b, 0:1],
                                             rstd[:, b:b + 1], ALU.subtract, ALU.mult)
                last.then_inc(ready, 1)

            def row_maxima(g, s, first):
                if not (first and s < 4):
                    dve.wait_ge(t_done, g * 2 - 6)
                for i in range(2):
                    dve.wait_ge(s_done, g * 2 + i + 1)
                    dve.sem_inc(dve_passed, 1)
                    for hd in range(2):
                        last = dve.tensor_tensor_reduce(
                            out=probs[:, s % 4, hd, SEQ * i:SEQ * i + KEYS[i]],
                            in0=s_ps[i][:, hd * KEYS[i]:(hd + 1) * KEYS[i]], in1=mask[:, M_OFF[i]:M_OFF[i] + KEYS[i]], scale=1.0,
                            scalar=MASKED, op0=ALU.add, op1=ALU.max,
                            accum_out=row_max[:, s % 4, 2 * hd + i:2 * hd + i + 1])
                    last.then_inc(max_done, 1)
                dve.wait_ge(max_done, g * 2 + 2)
                dve.tensor_scalar(neg_max[:, s % 4, :], row_max[:, s % 4, :], -SCALE, None,
                                  ALU.mult).then_inc(neg_ready, 1)

            def reciprocals(g, s):
                dve.wait_ge(exp_done, g + 1)
                dve.reciprocal(inv_sum[:, s % 4, :], row_sum[:, s % 4, :]).then_inc(inv_ready, 1)

            def evacuate(task, ps=qk_ps):
                kind, it, i = task
                if kind == "q":
                    dve.wait_ge(q_hi_ready, it * 8 + i + 1)
                    low(q_lo[:, i % 2, :], ps[:, :], q_hi[:, i % 2, :], B_QKV + i).then_inc(q_ready, 1)
                elif kind == "k":
                    for hd in range(2):
                        dve.wait_ge(k_hi_ready, it * 16 + 2 * i + hd + 1)
                        rows = slice(hd * HEAD_DIM, (hd + 1) * HEAD_DIM)
                        last = low(k_lo[rows, i % 2, hd, :], ps[rows, :], k_hi[rows, i % 2, hd, :],
                                   B_QKV + PAIRS + i, rows)
                    last.then_inc(k_ready, 1)
                elif kind == "tx":
                    dve.wait_ge(xnt_hi_ready, it + 1)
                    low(xnt_lo[:, :], misc[:, :], xnt_hi[:, :]).then_inc(xnt_ready, 1)
                elif kind == "m2":
                    dve.wait_ge(h_hi_ready, it + 1)
                    low(h_lo[:, :], misc[:, :], h_hi[:, :], B_2).then_inc(h_ready, 1)
                elif kind == "ty":
                    dve.wait_ge(ty_done, it + 1)
                    dve.tensor_tensor(x_group(it), misc[:, :], x_group(it), ALU.add).then_inc(x1_ready, 1)

            def silu_start(it):
                dve.wait_ge(e1_ready, it + 1)
                dve.tensor_scalar(z1[:, :], misc[:, :], bias[:, B_1:B_1 + 1], None,
                                  ALU.add).then_inc(z1_ready, 1)
                dve.tensor_scalar(e1[:, :], e1[:, :], 1.0, None, ALU.add).then_inc(silu_step, 1)

            def silu_reciprocal(it, n):
                a = e1[:, n * P:(n + 1) * P]
                if n == 0:
                    dve.wait_ge(silu_step, it * 4 - 2)
                last = dve.reciprocal(a, a)
                if n == BLOCKS - 1:
                    last.then_inc(silu_step, 1)

            def probs_t_out(g, s, first):
                dve.wait_ge(t_done, g * 2 + 2)
                if not (first and s < 2):
                    dve.wait_ge(pv_done, g - 1)
                dve.tensor_copy(probs_t[:, s % 2, 1, PT_FROM:], t_ps[1][:, PT_FROM:]).then_inc(pt_ready[1], 1)

            def group(it, first=False, last=False):
                for s in range(SLOTS):
                    g = it * SLOTS + s
                    row_maxima(g, s, first)
                    if not (first and s == 0):
                        reciprocals(g - 1, (s - 1) % SLOTS)
                    kind, ahead, i = task_a(s)
                    if not (last and ahead):
                        evacuate((kind, it + ahead, i))
                    b_task = TASK_B.get(s)
                    for now in (True, False):
                        if present(b_task, first, last) and now == (s in EARLY_B):
                            evacuate((b_task[0], it + b_task[1], b_task[2]))
                        if now and not (first and s < 2):
                            probs_t_out(g - 2, (s - 2) % SLOTS, first)
                    following = 0 if last else it + 1
                    if s == MOMENTS_AT and not first:
                        if last:
                            dve.wait_ge(x1_ready, 2)
                        moments(following, it + 1, stats_done, mv_ready)
                    if s == NORMAL_AT + 1 and first:
                        dve.wait_ge(x_rest_in, 16)
                    if s == NORMAL_AT:
                        normal_x(following, it + 1, rstd_ready, xn_ready)
                    if s == F_MOMENTS_AT and last:
                        moments(1, 0, f_stats, f_mv)
                    if s == F_NORMAL_AT and last:
                        normal_x(1, 0, f_rstd, f_xn)
                    if s == SILU_START and not last:
                        silu_start(it + 1)
                    for n in SILU_AT.get(s, ()) if not last else ():
                        silu_reciprocal(it + 1, n)

            dve.wait_ge(x_in, 16)
            moments(0, 0, stats_done, mv_ready)
            normal_x(0, 0, rstd_ready, xn_ready)
            dve.wait_ge(bias_in, 16)
            dve.tensor_scalar(neg_b1[:, :], bias[:, B_1:B_1 + 1], -1.0, None, ALU.mult)
            dve.wait_ge(w12_in, 32)
            dve.tensor_copy(w_hi[:, W_1:W_G], w_raw[:, W_1:W_G]).then_inc(w12_hi_ready, 1)
            dve.wait_ge(w12_hi_ready, 1)
            low(w_lo[:, W_1:W_G], w_raw[:, W_1:W_G], w_hi[:, W_1:W_G]).then_inc(w12_ready, 1)
            evacuate(("tx", 0, 0))
            silu_start(0)
            dve.wait_ge(silu_step, 1)
            for half in range(2):
                cols = slice(half * SEQ, half * SEQ + SEQ)
                dve.reciprocal(e1[:, cols], e1[:, cols]).then_inc(silu0_step, 1)
                dve.wait_ge(silu0_step, 2 * half + 1)
                dve.tensor_tensor(z1[:, cols], z1[:, cols], e1[:, cols], ALU.mult).then_inc(silu0_step, 1)
            for half in range(2):
                cols = slice(half * SEQ, half * SEQ + SEQ)
                dve.wait_ge(s0_hi_ready, half + 1)
                last = low(s_lo[:, cols], z1[:, cols], s_hi[:, cols])
            last.then_inc(s_ready, 1)
            dve.wait_ge(x_1_in, 16)
            moments(1, 1, stats_done, mv_ready)
            evacuate(("m2", 0, 0))
            evacuate(("k", 0, 0), FIRST_K_PS)
            evacuate(("q", 0, 0))
            evacuate(("q", 0, 1), FIRST_Q1_PS)
            dve.wait_ge(zeros_ready, 2)
            dve.wait_ge(consts_ready, 2)
            group(0, first=True)
            with dve.Fori(1, GROUPS - 1) as it:
                group(it)
            group(GROUPS - 1, last=True)
            n = GROUPS * SLOTS
            reciprocals(n - 1, SLOTS - 1)

            def f_xnt_out(c, odd):
                dve.wait_ge(f_xnt_hi, c)
                low(f_xnt_parts[odd][1], f_xt_ps[:, :], f_xnt_parts[odd][0]).then_inc(f_xnt, 1)

            def f_g_out(c, k):
                dve.wait_ge(f_g_hi, c * 3 + k + 1)
                low(o_lo[:, k, :], g_f32[k], o_hi[:, k, :]).then_inc(f_g, 1)

            def f_residual(c):
                dve.wait_ge(f_ty, c + 1)
                dve.tensor_tensor(x_group(c), f_yt_ps[:, :], x_group(c), ALU.add).then_inc(f_out, 1)

            def step(c, odd, left=3):
                if left >= 3:
                    dve.wait_ge(f_xn, c + 2)
                    moments(c + 3, c + 2, f_stats, f_mv)
                if left:
                    f_g_out(c + 1, 0)
                    f_g_out(c + 1, 1)
                if not (isinstance(c, int) and c < 1):
                    f_residual(c - 1)
                if left >= 2:
                    f_xnt_out(c + 2, odd)
                if left:
                    f_g_out(c + 1, 2)
                if left >= 3:
                    normal_x(c + 3, c + 2, f_rstd, f_xn)

            probs_t_out(n - 2, SLOTS - 2, False)
            f_xnt_out(1, 1)
            moments(2, 1, f_stats, f_mv)
            probs_t_out(n - 1, SLOTS - 1, False)
            normal_x(2, 1, f_rstd, f_xn)
            f_g_out(0, 0)
            evacuate(("ty", GROUPS - 1, 0))
            f_g_out(0, 1)
            f_g_out(0, 2)
            dve.wait_ge(x1_ready, GROUPS)
            f_steps(dve, step)
            f_residual(GROUPS - 1)


def kernel(**inputs):
    import numpy as _np
    import concourse.bacc as _bacc
    from concourse import mybir as _mybir
    from concourse.bass_utils import run_bass_kernel_spmd as _run

    a = {k: _np.asarray(t) for k, t in inputs.items()}
    n, dim = BATCH * SEQ, DIM

    def columns(t):
        return t.reshape(-1, P).T

    arrays = {
        "x": a["L0_attn_x"].reshape(n, dim),
        "w1t": a["L0_attn_W1"].T,
        "w2t": a["L0_attn_W2"].T,
        "wgt": a["L0_attn_Wg"].T,
        "wot": a["L0_attn_Wo"].T.reshape(PAIRS, P, dim).transpose(1, 0, 2).reshape(P, PAIRS * dim),
        "fw1": a["L0_ffn_w1"],
        "fw2": a["L0_ffn_w2"].reshape(HCHUNKS, P, dim).transpose(1, 0, 2).reshape(P, HCHUNKS * dim),
        "biases": _np.concatenate([columns(a[k]) for k in (
            "L0_attn_bg", "L0_attn_b1", "L0_attn_b2", "L0_attn_bo", "L0_ffn_b1", "L0_ffn_b2")], axis=1),
    }
    arrays = {k: _np.ascontiguousarray(t) for k, t in arrays.items()}
    nc = _bacc.Bacc("TRN2", target_bir_lowering=False, num_devices=1)
    args = [nc.dram_tensor(f"in_{k}", t.shape, _mybir.dt.from_np(t.dtype), kind="ExternalInput").ap()
            for k, t in arrays.items()]
    out = nc.dram_tensor("out_0", (n, dim), F32, kind="ExternalOutput").ap()
    preln_block(nc, *args, out)
    r = _run(nc, [{f"in_{k}": t for k, t in arrays.items()}], core_ids=[0])
    return r.results[0]["out_0"].reshape(BATCH, SEQ, DIM)
```
